# Optimizing a Trainium2 kernel written in Bass

```python
import numpy as np
import jax
import jax.numpy as jnp

def _softmax(x, axis=-1):
    return jax.nn.softmax(x, axis=axis)

def _gelu(x):
    return jax.nn.gelu(x, approximate=True)

def _silu(x):
    return jax.nn.silu(x)

def _sigmoid(x):
    return jax.nn.sigmoid(x)

def _layernorm(x, axis=-1, eps=1e-05):
    m = jnp.mean(x, axis=axis, keepdims=True)
    v = jnp.var(x, axis=axis, keepdims=True)
    return (x - m) / jnp.sqrt(v + eps)

def _scatter_add(tgt, idx, src, axis=0):
    return tgt.at[idx].add(src)

def _segment_sum(src, seg, n):
    return jax.ops.segment_sum(src, seg, n)
kernel_name = 'mk_gnn_resnorm_d2_gnn_r8_0c4797'

def setup_inputs(seed: int=0):
    np.random.seed(seed)
    _w = jnp.asarray

    def _rec_inputs():
        import jax
        import jax.numpy as jnp
        _gk = jax.random.key(seed)
        x = -0.0003713 + 1 * jax.random.normal(jax.random.fold_in(_gk, 1), (6250, 128), jnp.float32)
        _s = jax.random.randint(jax.random.fold_in(_gk, 2), (50000,), 0, 6250, jnp.int32)
        _d = jax.random.randint(jax.random.fold_in(_gk, 3), (50000,), 0, 6250, jnp.int32)
        _loop = jnp.arange(6250, dtype=jnp.int32)
        src = jnp.concatenate([_s, _d, _loop])
        dst = jnp.concatenate([_d, _s, _loop])
        _o = jnp.argsort(dst, stable=True)
        src = src[_o]
        dst = dst[_o]
        edge_type_4 = jax.random.randint(jax.random.fold_in(_gk, 12), (106250,), 0, 4, jnp.int32)
        edge_weight = jax.random.uniform(jax.random.fold_in(_gk, 13), (106250,), jnp.float32, 0.0, 0.999996)
        return (x, src, dst, edge_type_4, edge_weight)
    x, src, dst, edge_type_4, edge_weight = _rec_inputs()

    def _L0_gnn_setup():
        import jax, jax.numpy as jnp
        import numpy as np
        N_NODES = 12500
        N_EDGES = 200000
        D_IN = 128
        D_HID = 128

        def _gcn_norm(edge_index, num_nodes):
            loop = jnp.arange(num_nodes, dtype=edge_index.dtype)
            src = jnp.concatenate([edge_index[0], loop])
            dst = jnp.concatenate([edge_index[1], loop])
            deg = jax.ops.segment_sum(jnp.ones_like(dst, dtype=jnp.float32), dst, num_segments=num_nodes)
            dis = jnp.where(deg > 0, jax.lax.rsqrt(deg), 0.0)
            norm = dis[src] * dis[dst]
            return (src, dst, norm)

        def _gcn_conv(x, src, dst, norm, W, b, num_nodes):
            h = x @ W
            msg = h[src] * norm[:, None]
            out = jax.ops.segment_sum(msg, dst, num_segments=num_nodes)
            return out + b
        key = jax.random.key(seed)
        ks = jax.random.split(key, 9)
        x = jax.random.normal(ks[0], (N_NODES, D_IN), dtype=jnp.float32)
        edge_index = jax.random.randint(ks[1], (2, N_EDGES), 0, N_NODES, dtype=jnp.int64)
        s = 1.0 / np.sqrt(D_IN)
        W0 = jax.random.uniform(ks[2], (D_IN, D_HID), jnp.float32, -s, s)
        W1 = jax.random.uniform(ks[3], (D_HID, D_HID), jnp.float32, -s, s)
        W2 = jax.random.uniform(ks[4], (D_HID, D_HID), jnp.float32, -s, s)
        b0 = jax.random.uniform(ks[5], (D_HID,), jnp.float32, -s, s)
        b1 = jax.random.uniform(ks[6], (D_HID,), jnp.float32, -s, s)
        b2 = jax.random.uniform(ks[7], (D_HID,), jnp.float32, -s, s)
        return {'x': x, 'edge_index': edge_index, 'W0': W0, 'W1': W1, 'W2': W2, 'b0': b0, 'b1': b1, 'b2': b2}
    _L0_gnn_all = _L0_gnn_setup()
    _L0_gnn_in = {k: v for k, v in _L0_gnn_all.items() if k in ('W0', 'W1', 'W2', 'b0', 'b1', 'b2')}
    del _L0_gnn_all

    def _L1_gnn_setup():
        import jax, jax.numpy as jnp
        import numpy as np
        NUM_RELATIONS = 4
        N_NODES = 2500
        N_EDGES = 40000
        F_IN = 128
        HID = 128
        EMB = 128

        def _rgcn_conv(x, src, dst, edge_type, edge_weight, W, root, bias):
            xj = x[src]
            m = jnp.zeros((xj.shape[0], W.shape[2]), dtype=x.dtype)
            for r in range(W.shape[0]):
                mask = (edge_type == r).astype(x.dtype)[:, None]
                m = m + mask * (xj @ W[r])
            m = m * edge_weight[:, None]
            out = jax.ops.segment_sum(m, dst, num_segments=x.shape[0])
            return out + x @ root + bias
        key = jax.random.key(seed)
        ks = jax.random.split(key, 10)
        return {'x': jax.random.normal(ks[0], (N_NODES, F_IN), dtype=jnp.float32), 'edge_index': jax.random.randint(ks[1], (2, N_EDGES), 0, N_NODES, dtype=jnp.int64 if jax.config.jax_enable_x64 else jnp.int32).astype(jnp.int32), 'edge_type': jax.random.randint(ks[2], (N_EDGES,), 0, NUM_RELATIONS).astype(jnp.int32), 'edge_weight': jax.random.uniform(ks[3], (N_EDGES,), dtype=jnp.float32), 'W1': jax.random.normal(ks[4], (NUM_RELATIONS, F_IN, HID), dtype=jnp.float32) * 0.05, 'root1': jax.random.normal(ks[5], (F_IN, HID), dtype=jnp.float32) * 0.05, 'b1': jax.random.normal(ks[6], (HID,), dtype=jnp.float32) * 0.05, 'W2': jax.random.normal(ks[7], (NUM_RELATIONS, HID, EMB), dtype=jnp.float32) * 0.05, 'root2': jax.random.normal(ks[8], (HID, EMB), dtype=jnp.float32) * 0.05, 'b2': jax.random.normal(ks[9], (EMB,), dtype=jnp.float32) * 0.05}
    _L1_gnn_all = _L1_gnn_setup()
    _L1_gnn_in = {k: v for k, v in _L1_gnn_all.items() if k in ('W1', 'root1', 'b1', 'W2', 'root2', 'b2')}
    del _L1_gnn_all
    return {'x': x, 'src': src, 'dst': dst, 'edge_type_4': edge_type_4, 'edge_weight': edge_weight, 'L0_gnn_W0': _L0_gnn_in['W0'], 'L0_gnn_W1': _L0_gnn_in['W1'], 'L0_gnn_W2': _L0_gnn_in['W2'], 'L0_gnn_b0': _L0_gnn_in['b0'], 'L0_gnn_b1': _L0_gnn_in['b1'], 'L0_gnn_b2': _L0_gnn_in['b2'], 'L1_gnn_W1': _L1_gnn_in['W1'], 'L1_gnn_root1': _L1_gnn_in['root1'], 'L1_gnn_b1': _L1_gnn_in['b1'], 'L1_gnn_W2': _L1_gnn_in['W2'], 'L1_gnn_root2': _L1_gnn_in['root2'], 'L1_gnn_b2': _L1_gnn_in['b2']}

def reference(x, src, dst, edge_type_4, edge_weight, L0_gnn_W0, L0_gnn_W1, L0_gnn_W2, L0_gnn_b0, L0_gnn_b1, L0_gnn_b2, L1_gnn_W1, L1_gnn_root1, L1_gnn_b1, L1_gnn_W2, L1_gnn_root2, L1_gnn_b2):
    import jax
    import jax.numpy as jnp

    def _L0_gnn_ref(x, edge_index, W0, W1, W2, b0, b1, b2):
        import jax, jax.numpy as jnp
        import numpy as np
        N_NODES = 12500
        N_EDGES = 200000
        D_IN = 128
        D_HID = 128

        def _gcn_norm(edge_index, num_nodes):
            loop = jnp.arange(num_nodes, dtype=edge_index.dtype)
            src = jnp.concatenate([edge_index[0], loop])
            dst = jnp.concatenate([edge_index[1], loop])
            deg = jax.ops.segment_sum(jnp.ones_like(dst, dtype=jnp.float32), dst, num_segments=num_nodes)
            dis = jnp.where(deg > 0, jax.lax.rsqrt(deg), 0.0)
            norm = dis[src] * dis[dst]
            return (src, dst, norm)

        def _gcn_conv(x, src, dst, norm, W, b, num_nodes):
            h = x @ W
            msg = h[src] * norm[:, None]
            out = jax.ops.segment_sum(msg, dst, num_segments=num_nodes)
            return out + b
        n = x.shape[0]
        src, dst, norm = _gcn_norm(edge_index, n)
        h = jax.nn.relu(_gcn_conv(x, src, dst, norm, W0, b0, n))
        h = jax.nn.relu(_gcn_conv(h, src, dst, norm, W1, b1, n))
        h = jax.nn.relu(_gcn_conv(h, src, dst, norm, W2, b2, n))
        return jax.nn.log_softmax(h, axis=1)

    def _L1_gnn_ref(x, edge_index, edge_type, edge_weight, W1, root1, b1, W2, root2, b2):
        import jax, jax.numpy as jnp
        import numpy as np
        NUM_RELATIONS = 4
        N_NODES = 2500
        N_EDGES = 40000
        F_IN = 128
        HID = 128
        EMB = 128

        def _rgcn_conv(x, src, dst, edge_type, edge_weight, W, root, bias):
            xj = x[src]
            m = jnp.zeros((xj.shape[0], W.shape[2]), dtype=x.dtype)
            for r in range(W.shape[0]):
                mask = (edge_type == r).astype(x.dtype)[:, None]
                m = m + mask * (xj @ W[r])
            m = m * edge_weight[:, None]
            out = jax.ops.segment_sum(m, dst, num_segments=x.shape[0])
            return out + x @ root + bias
        src, dst = (edge_index[0], edge_index[1])
        ew = (edge_weight - edge_weight.min()) / (edge_weight.max() - edge_weight.min() + 1e-08)
        h = jax.nn.relu(_rgcn_conv(x, src, dst, edge_type, ew, W1, root1, b1))
        h = _rgcn_conv(h, src, dst, edge_type, ew, W2, root2, b2)
        return h
    edge_index = jnp.stack([src, dst])
    x = _layernorm(x + _L0_gnn_ref(x, edge_index, L0_gnn_W0, L0_gnn_W1, L0_gnn_W2, L0_gnn_b0, L0_gnn_b1, L0_gnn_b2), axis=-1)
    x = _layernorm(x + _L1_gnn_ref(x, edge_index, edge_type_4, edge_weight, L1_gnn_W1, L1_gnn_root1, L1_gnn_b1, L1_gnn_W2, L1_gnn_root2, L1_gnn_b2), axis=-1)
    return x

_drawn_inputs = setup_inputs


def setup_inputs(seed=0):
    import zlib

    import numpy as np

    out = dict(_drawn_inputs(seed))
    spreads = {}
    factors = {'L0_gnn_W0': 25.618, 'L0_gnn_b0': 6.319}
    for name, (base, spread) in spreads.items():
        noise = np.random.default_rng([zlib.crc32(name.encode()), seed]).standard_normal(out[name].shape)
        drawn = base * np.exp(spread * noise) if base else spread * noise
        out[name] = jnp.asarray(drawn.astype(out[name].dtype))
    for name, factor in factors.items():
        out[name] = (out[name] * factor).astype(out[name].dtype)
    return out
```

```python
from contextlib import ExitStack

import concourse.bass as bass
from concourse import mybir

P = 128
N_NODES = 6250
N_EDGES = 106250
F = 128
R = 4
GCN_LAYERS = 3

NODE_TILES = -(-N_NODES // P)
NODES = NODE_TILES * P
CT = 7
CHUNKS = NODE_TILES // CT
CN = CT * P
HALF = CN // 2
LAST_ROWS = N_NODES - (NODE_TILES - 1) * P

G = 4
U = 4
SLOTS = G * U
TURNS = -(-N_EDGES // (P * SLOTS))
GROUPS = TURNS * U
TILES = TURNS * SLOTS
WIN = 64
WIDE = 512
WIDES = -(-NODES // WIDE)
ACC = WIDES * WIDE

EPS = 1e-5

F32 = mybir.dt.float32
BF16 = mybir.dt.bfloat16
I32 = mybir.dt.int32
ALU = mybir.AluOpType
ACT = mybir.ActivationFunctionType
AX = mybir.AxisListType


def build(nc, x, src, dst, first_dst, edge_type, weight, gcn_w, gcn_b, rel_w1, rel_w2, rel_root, rel_b, out):
    gcn_table = nc.dram_tensor("gcn_table", [NODES, F], F32, kind="Internal").ap()
    rel_table = nc.dram_tensor("rel_table", [NODES * R, F], F32, kind="Internal").ap()

    ctx = ExitStack()
    with ctx:
        def sb(name, shape, dt=F32):
            return ctx.enter_context(nc.sbuf_tensor(name, shape, dt))

        def sem(name):
            return ctx.enter_context(nc.semaphore(name))

        src_i = sb("src_i", [P, TILES], I32)
        type_i = sb("type_i", [P, TILES], I32)
        rel_i = sb("rel_i", [P, TILES], I32)
        dst_f = sb("dst_f", [P, TILES])
        off_f = sb("off_f", [P, TILES])
        w_f = sb("w_f", [P, TILES])
        first_i = sb("first_i", [1, GROUPS], I32)
        first_f = sb("first_f", [1, GROUPS])
        slow_i = sb("slow_i", [1, 1], I32)
        xres = sb("xres", [P, NODE_TILES, F])
        hT = sb("hT", [P, NODES])
        acc = sb("acc", [P, ACC])
        dis = sb("dis", [P, NODES])
        tab = sb("tab", [P, NODES])
        gcn_rows = tab[:, :].rearrange("p (t f) -> p t f", f=F)
        rel_rows = tab[:, 0:CT * R * F].rearrange("p (t f) -> p t f", f=R * F)
        idx = sb("idx", [P, SLOTS], I32)
        rows = sb("rows", [P, SLOTS, F])
        onehot = sb("onehot", [P, U, G, WIN])
        onehot_b = sb("onehot_b", [P, U, G, WIN], BF16)
        work = sb("work", [P, 2, CN])
        wide = hT[:, 0:G * WIDE].rearrange("p (q n) -> p q n", q=G)
        iota_i = sb("iota_i", [P, WIDE], I32)
        iota = sb("iota", [P, WIDE])
        wstart = sb("wstart", [P, WIDES])
        ident = sb("ident", [P, P])
        ones = sb("ones", [P, P])
        ones_b = sb("ones_b", [P, P], BF16)
        wg = sb("wg", [P, GCN_LAYERS, F])
        bg = sb("bg", [P, GCN_LAYERS])
        wr = sb("wr", [P, 2, R, F])
        rr = sb("rr", [P, 2, F])
        br = sb("br", [P, 2])
        small = sb("small", [P, 6, 8])
        mx, ssum, lnsum, mean, var, rstd = (small[:, k, 0:CT] for k in range(6))
        ext = sb("ext", [P, 2])
        ext_all = sb("ext_all", [P, 2])
        span = sb("span", [P, 4])
        inwin = sb("inwin", [P, 2])

        pa = ctx.enter_context(nc.psum_tensor("pa", [P, 2, 512], F32))
        pb = ctx.enter_context(nc.psum_tensor("pb", [P, 2, 512], F32))
        pc = ctx.enter_context(nc.psum_tensor("pc", [P, 2, 512], F32))
        pw = ctx.enter_context(nc.psum_tensor("pw", [P, 2, 512], F32))
        pa_t = pa[:, :, :].rearrange("p a n -> p (a n)")[:, 0:CN].rearrange("p (t f) -> p t f", f=F)
        pb_t = pb[:, :, :].rearrange("p a n -> p (a n)")[:, 0:CN].rearrange("p (t f) -> p t f", f=F)

        def window(u):
            return (pw if u < 2 else pb)[:, u % 2, 0:WIN]

        loaded_edges = sem("loaded_edges")
        loaded_x = sem("loaded_x")
        loaded_w = sem("loaded_w")
        consts_made = sem("consts_made")
        dve_step = sem("dve_step")
        ext_ready = sem("ext_ready")
        ext_reduced = sem("ext_reduced")
        first_cast = sem("first_cast")
        first_spread = sem("first_spread")
        inwin_ready = sem("inwin_ready")
        inwin_summed = sem("inwin_summed")
        flag_ready = sem("flag_ready")
        consts_ready = sem("consts_ready")
        rel_ready = sem("rel_ready")
        idx_ready = sem("idx_ready")
        row_landed = [sem(f"row_landed{k}") for k in range(SLOTS)]
        onehot_ready = sem("onehot_ready")
        group_summed = sem("group_summed")
        window_added = sem("window_added")
        wide_ready = sem("wide_ready")
        wide_summed = sem("wide_summed")
        wide_added = sem("wide_added")
        hot_built = sem("hot_built")
        wide_built = sem("wide_built")
        layer_summed = sem("layer_summed")
        root_ready = sem("root_ready")
        dis_ready = sem("dis_ready")
        scaled = sem("scaled")
        relued = sem("relued")
        h_ready = sem("h_ready")
        a_full = sem("a_full")
        a_free = sem("a_free")
        b_full = sem("b_full")
        b_free = sem("b_free")
        bt_full = sem("bt_full")
        bt_free = sem("bt_free")
        c_full = sem("c_full")
        c_free = sem("c_free")
        rows_filled = sem("rows_filled")
        rows_stored = sem("rows_stored")
        rel_filled = sem("rel_filled")
        rel_stored = [sem(f"rel_stored{j}") for j in range(CT)]
        rel_free = sem("rel_free")
        acc_ready = sem("acc_ready")
        z_ready = sem("z_ready")
        exp_done = sem("exp_done")
        s_ready = sem("s_ready")
        ln_done = sem("ln_done")
        y_ready = sem("y_ready")
        sq_done = sem("sq_done")
        v_ready = sem("v_ready")
        sd_done = sem("sd_done")
        x1_ready = sem("x1_ready")
        out_ready = sem("out_ready")
        out_stored = sem("out_stored")

        PHASES = 1 + GCN_LAYERS + 2

        block = ctx.enter_context(nc.Block())

        @block.sync
        def _(sp):
            sp.sem_inc(rel_free, CT)
            for tile_, arr in ((dst_f[:, :].bitcast(I32), dst), (w_f[:, :], weight)):
                sp.dma_start(tile_, arr).then_inc(loaded_edges, 16)
            sp.dma_start(first_i[:, :], first_dst).then_inc(loaded_edges, 16)
            sp.dma_start(src_i[:, :], src).then_inc(loaded_edges, 16)
            sp.dma_start(type_i[:, :], edge_type).then_inc(loaded_edges, 16)
            sp.dma_start(xres[:, :, :], x.rearrange("(t p) f -> p t f", p=P)).then_inc(loaded_x, 16)
            sp.dma_start(wg[:, :, :], gcn_w.rearrange("l i o -> i l o")).then_inc(loaded_w, 16)
            sp.dma_start(bg[:, :], gcn_b).then_inc(loaded_w, 16)
            sp.dma_start(wr[:, 0, :, :], rel_w1.rearrange("r i o -> i r o")).then_inc(loaded_w, 16)
            sp.dma_start(wr[:, 1, :, :], rel_w2.rearrange("r i o -> i r o")).then_inc(loaded_w, 16)
            sp.dma_start(rr[:, :, :], rel_root.rearrange("l i o -> i l o")).then_inc(loaded_w, 16)
            sp.dma_start(br[:, :], rel_b).then_inc(loaded_w, 16)

            gcn_out = gcn_table.rearrange("(c t p) f -> c p t f", p=P, t=CT)
            for d in range(GCN_LAYERS):
                with sp.Fori(0, CHUNKS) as c:
                    sp.wait_ge(rows_filled, c + (CHUNKS * d + 1))
                    sp.dma_start(gcn_out[bass.ds(c, 1)].rearrange("a p t f -> p (a t) f"),
                                 gcn_rows[:, bass.ds(c * CT, CT), :]).then_inc(rows_stored, 16)
            rel_out = rel_table.rearrange("(c t p r) f -> (c t) p (r f)", p=P, t=CT, r=R)
            for d in range(2):
                with sp.Fori(0, CHUNKS) as c:
                    for j in range(CT):
                        sp.wait_ge(rel_filled, c * CT + (NODE_TILES * d + j + 1))
                        sp.dma_start(rel_out[bass.ds(c * CT + j, 1)].rearrange("a p f -> (a p) f"),
                                     rel_rows[:, j, :]).then_inc(rel_stored[j], 16)
                    for j in range(CT):
                        sp.wait_ge(rel_stored[j], c * 16 + 16 * (CHUNKS * d + 1))
                        sp.sem_inc(rel_free, 1)
            out_v = out[0:(NODE_TILES - 1) * P, :].rearrange("(t p) f -> p t f", p=P)
            with sp.Fori(0, CHUNKS - 1) as c:
                sp.wait_ge(out_ready, c + 1)
                sp.dma_start(out_v[:, bass.ds(c * CT, CT), :], xres[:, bass.ds(c * CT, CT), :])\
                  .then_inc(out_stored, 16)
            sp.wait_ge(out_ready, CHUNKS)
            t0 = (CHUNKS - 1) * CT
            sp.dma_start(out_v[:, t0:NODE_TILES - 1, :], xres[:, t0:NODE_TILES - 1, :]).then_inc(out_stored, 16)
            sp.dma_start(out[(NODE_TILES - 1) * P:N_NODES, :], xres[0:LAST_ROWS, NODE_TILES - 1, :])\
              .then_inc(out_stored, 16)
            sp.wait_ge(out_stored, 16 * (CHUNKS + 1))

        @block.gpsimd
        def _(pool):
            pool.iota(iota_i[:, :], pattern=[[1, WIDE]], base=0, channel_multiplier=0).then_inc(consts_made, 1)
            pool.memset(ident[:, :], 0.0).then_inc(consts_made, 1)
            pool.wait_ge(consts_made, 2)
            pool.affine_select(out=ident[:, :], in_=ident[:, :], compare_op=ALU.not_equal, fill=1.0,
                               base=0, pattern=[[-1, P]], channel_multiplier=1).then_inc(consts_made, 1)
            pool.wait_ge(ext_ready, 1)
            pool.partition_all_reduce(ext_all[:, :], ext[:, :], P, bass.bass_isa.ReduceOp.max)\
                .then_inc(ext_reduced, 1)

            for phase in range(1, PHASES):
                layer = phase - 1
                if layer < GCN_LAYERS:
                    table = gcn_table
                    pool.wait_ge(rows_stored, 16 * CHUNKS * (layer + 1))
                else:
                    table = rel_table
                    pool.wait_ge(rel_free, CT + NODE_TILES * (layer - GCN_LAYERS + 1))
                with pool.Fori(0, TURNS) as i:
                    for k in range(SLOTS):
                        if k % (SLOTS // 2) == 0:
                            pool.wait_ge(idx_ready, i * 2 + (2 * TURNS * layer + k // (SLOTS // 2) + 1))
                        if k % G == 0:
                            pool.wait_ge(group_summed, i * U + (GROUPS * phase + k // G + 1))
                        if k % G == 0:
                            pool.nop(nofuse=True)
                        pool.indirect_dma_start(
                            out=rows[:, k, :], out_offset=None, in_=table,
                            in_offset=bass.IndirectOffsetOnAxis(ap=idx[:, k:k + 1], axis=0),
                        ).then_inc(row_landed[k], 16)

        @block.scalar
        def _(act):
            act.sem_inc(b_free, 1)
            act.sem_inc(bt_free, 2)
            act.sem_inc(c_free, 1)
            act.wait_ge(loaded_edges, 16 * 5)
            act.wait_ge(loaded_w, 16 * 6)

            with act.Fori(0, CHUNKS) as c:
                act.wait_ge(scaled, c + 1)
                act.nop(nofuse=True)
                act.activation(hT[:, bass.ds(c * CN, CN)], hT[:, bass.ds(c * CN, CN)], ACT.Sqrt)\
                   .then_inc(root_ready, 1)

            def copy_indices(table_rows, layer):
                half = SLOTS // 2
                with act.Fori(0, TURNS) as i:
                    for h in range(2):
                        act.wait_ge(group_summed, i * U + (GROUPS * (layer + 1) + (h + 1) * U // 2))
                        act.nop(nofuse=True)
                        act.activation(idx[:, h * half:(h + 1) * half],
                                       table_rows[:, bass.ds(i * SLOTS + h * half, half)], ACT.Copy)\
                           .then_inc(idx_ready, 1)

            def own_term(c, n, bias):
                act.wait_ge(c_full, n + 1)
                if bias is None:
                    act.nop(nofuse=True)
                    act.activation(acc[:, bass.ds(c * CN, CN)].rearrange("p (a n) -> p a n", a=2),
                                   pc[:, :, 0:HALF], ACT.Copy).then_inc(acc_ready, 1)
                else:
                    act.nop(nofuse=True)
                    act.activation(acc[:, bass.ds(c * CN, CN)].rearrange("p (a n) -> p a n", a=2),
                                   pc[:, :, 0:HALF], ACT.Identity, bias=bias).then_inc(acc_ready, 1)
                act.wait_ge(acc_ready, n + 1)
                act.sem_inc(c_free, 1)

            def rel_rows_out(c, d):
                for j in range(CT):
                    act.wait_ge(bt_full, c * CT + (NODE_TILES * d + j + 1))
                    act.wait_ge(rel_free, c * CT + (NODE_TILES * d + j + 1))
                    act.nop(nofuse=True)
                    act.activation(rel_rows[:, j, :], pb[:, j % 2, :], ACT.Copy).then_inc(rel_filled, 1)
                    act.wait_ge(rel_filled, c * CT + (NODE_TILES * d + j + 1))
                    act.sem_inc(bt_free, 1)

            for d in range(GCN_LAYERS):
                with act.Fori(0, CHUNKS) as c:
                    chunk = hT[:, bass.ds(c * CN, CN)]
                    if d > 0:
                        act.wait_ge(scaled, c + (CHUNKS * d + 1))
                        act.nop(nofuse=True)
                        act.activation(chunk, chunk, ACT.Relu, bias=bg[:, d - 1:d]).then_inc(relued, 1)
                    act.wait_ge(b_full, c + (CHUNKS * d + 1))
                    act.nop(nofuse=True)
                    act.activation(gcn_rows[:, bass.ds(c * CT, CT), :], pb_t, ACT.Copy).then_inc(rows_filled, 1)
                    act.wait_ge(rows_filled, c + (CHUNKS * d + 1))
                    act.sem_inc(b_free, 1)
                    own_term(c, c + CHUNKS * d, None)
                copy_indices(src_i, d)

            with act.Fori(0, CHUNKS) as c:
                chunk = hT[:, bass.ds(c * CN, CN)]
                z, e = (work[:, k, :] for k in range(2))
                act.wait_ge(scaled, c + (CHUNKS * GCN_LAYERS + 1))
                act.nop(nofuse=True)
                act.activation(chunk, chunk, ACT.Relu, bias=bg[:, GCN_LAYERS - 1:GCN_LAYERS]).then_inc(relued, 1)
                act.wait_ge(z_ready, c + 1)
                act.nop(nofuse=True)
                act.activation(e, z, ACT.Exp).then_inc(exp_done, 1)
                act.wait_ge(s_ready, c + 1)
                act.nop(nofuse=True)
                act.activation(lnsum, ssum, ACT.Ln).then_inc(ln_done, 1)
                act.wait_ge(y_ready, c + 1)
                act.nop(nofuse=True)
                act.activation(e, z, ACT.Square).then_inc(sq_done, 1)
                act.wait_ge(v_ready, c + 1)
                act.nop(nofuse=True)
                act.activation(rstd, var, ACT.Sqrt).then_inc(sd_done, 1)
                act.wait_ge(a_full, c * 2 + (CHUNKS + 2))
                act.nop(nofuse=True)
                act.activation(chunk.rearrange("p (t n) -> p t n", n=P), pa_t, ACT.Copy).then_inc(h_ready, 1)
                act.wait_ge(h_ready, c + (CHUNKS * GCN_LAYERS + 1))
                act.sem_inc(a_free, 1)
                rel_rows_out(c, 0)
                own_term(c, c + CHUNKS * GCN_LAYERS, br[:, 0:1])
            copy_indices(rel_i, GCN_LAYERS)

            with act.Fori(0, CHUNKS) as c:
                act.wait_ge(layer_summed, PHASES - 1)
                act.nop(nofuse=True)
                act.activation(hT[:, bass.ds(c * CN, CN)], acc[:, bass.ds(c * CN, CN)], ACT.Relu)\
                   .then_inc(h_ready, 1)
                rel_rows_out(c, 1)
                own_term(c, c + CHUNKS * (GCN_LAYERS + 1), br[:, 1:2])
            copy_indices(rel_i, GCN_LAYERS + 1)

            with act.Fori(0, CHUNKS) as c:
                act.wait_ge(y_ready, c + (CHUNKS + 1))
                act.nop(nofuse=True)
                act.activation(work[:, 1, :], work[:, 0, :], ACT.Square).then_inc(sq_done, 1)
                act.wait_ge(v_ready, c + (CHUNKS + 1))
                act.nop(nofuse=True)
                act.activation(rstd, var, ACT.Sqrt).then_inc(sd_done, 1)

        @block.vector
        def _(v):
            steps = [0]

            def then(ins):
                steps[0] += 1
                ins.then_inc(dve_step, 1)
                v.wait_ge(dve_step, steps[0])

            v.sem_inc(a_free, 1)
            v.sem_inc(window_added, U)
            v.sem_inc(wide_added, 1)
            v.memset(ones[:, :], 1.0)
            v.memset(ones_b[:, :], 1.0)
            then(v.memset(acc[:, :], 0.0))
            v.wait_ge(consts_made, 3)
            v.tensor_copy(iota[:, :], iota_i[:, :])
            then(v.tensor_scalar(wstart[:, :], iota_i[:, 0:WIDES], float(WIDE), None, ALU.mult))

            v.wait_ge(loaded_edges, 16 * 5)
            v.tensor_copy(first_f[:, :], first_i[:, :]).then_inc(first_cast, 1)
            then(v.tensor_copy(off_f[:, :], dst_f[:, :].bitcast(I32)))
            then(v.tensor_copy(dst_f[:, :], off_f[:, :]))

            v.tensor_copy(off_f[:, :], src_i[:, :])
            then(v.tensor_copy(work[:, 0, 0:TILES], type_i[:, :]))
            then(v.scalar_tensor_tensor(rel_i[:, :], off_f[:, :], float(R), work[:, 0, 0:TILES],
                                        op0=ALU.mult, op1=ALU.add))
            then(v.tensor_reduce(ext[:, 0:1], w_f[:, :], AX.X, ALU.min))
            then(v.tensor_scalar(ext[:, 0:1], ext[:, 0:1], -1.0, None, ALU.mult))
            v.tensor_reduce(ext[:, 1:2], w_f[:, :], AX.X, ALU.max).then_inc(ext_ready, 1)
            v.wait_ge(ext_reduced, 1)
            then(v.tensor_tensor(span[:, 0:1], ext_all[:, 0:1], ext_all[:, 1:2], ALU.add))
            then(v.tensor_scalar(span[:, 1:2], span[:, 0:1], 1e-8, None, ALU.add))
            then(v.reciprocal(span[:, 2:3], span[:, 1:2]))
            then(v.tensor_scalar(w_f[:, :], w_f[:, :], ext_all[:, 0:1], span[:, 2:3], ALU.add, ALU.mult))

            v.wait_ge(first_spread, 1)
            then(v.tensor_copy(work[:, 1, 0:GROUPS], pc[:, 0, 0:GROUPS]))
            then(v.tensor_tensor(off_f[:, :].rearrange("p (g k) -> p g k", k=G),
                                 dst_f[:, :].rearrange("p (g k) -> p g k", k=G),
                                 work[:, 1, 0:GROUPS].unsqueeze(2).to_broadcast([P, GROUPS, G]), ALU.subtract))
            then(v.tensor_scalar(work[:, 0, 0:TILES], off_f[:, :], 0.0, None, ALU.is_ge))
            then(v.scalar_tensor_tensor(work[:, 0, 0:TILES], off_f[:, :], float(WIN), work[:, 0, 0:TILES],
                                        op0=ALU.is_lt, op1=ALU.mult))
            v.tensor_reduce(inwin[:, 0:1], work[:, 0, 0:TILES], AX.X, ALU.add).then_inc(inwin_ready, 1)
            v.wait_ge(inwin_summed, 1)
            v.tensor_scalar(slow_i[0:1, 0:1], pc[0:1, 1, 0:1], -1.0, float(N_EDGES), ALU.mult, ALU.add)\
             .then_inc(flag_ready, 1)
            v.wait_ge(flag_ready, 1)
            slow = v.value_load(slow_i[0:1, 0:1], min_val=0, max_val=N_EDGES)


            def aggregate(phase):
                weighted = phase > GCN_LAYERS
                ring = onehot_b if phase == 0 else onehot
                done = GROUPS * phase
                weighted_done = GROUPS * (phase - GCN_LAYERS - 1)
                if phase > 0:
                    v.wait_ge(acc_ready, CHUNKS * phase)
                with v.If(slow == 0):
                    with v.Fori(0, TURNS) as i:
                        firsts = [v.value_load(first_i[0:1, bass.ds(i * U + u, 1)], min_val=0, max_val=N_NODES - 1)
                                  for u in range(U)]
                        for u in range(U):
                            off = off_f[:, bass.ds(i * SLOTS + u * G, G)].unsqueeze(2).to_broadcast([P, G, WIN])
                            nodes = iota[:, 0:WIN].unsqueeze(1).to_broadcast([P, G, WIN])
                            v.wait_ge(group_summed, i * U + (done + u + 1))
                            if weighted:
                                w = w_f[:, bass.ds(i * SLOTS + u * G, G)].unsqueeze(2).to_broadcast([P, G, WIN])
                                v.tensor_tensor(ring[:, u], off, nodes, ALU.is_equal).then_inc(hot_built, 1)
                                v.wait_ge(hot_built, i * U + (weighted_done + u + 1))
                                v.tensor_tensor(ring[:, u], ring[:, u], w, ALU.mult).then_inc(onehot_ready, 1)
                            else:
                                v.tensor_tensor(ring[:, u], off, nodes, ALU.is_equal).then_inc(onehot_ready, 1)
                        for u in range(U):
                            nodes = acc[:, bass.ds(firsts[u], WIN)]
                            v.wait_ge(group_summed, i * U + (done + U + u + 1))
                            v.wait_ge(window_added, i * U + (done + U + u))
                            v.tensor_tensor(nodes, nodes, window(u), ALU.add).then_inc(window_added, 1)
                    v.wait_ge(window_added, done + GROUPS + U)
                with v.Else():
                    with v.Fori(0, GROUPS) as g:
                        with v.Fori(0, WIDES) as b:
                            dst_g = dst_f[:, bass.ds(g * G, G)].unsqueeze(2).to_broadcast([P, G, WIDE])
                            nodes = iota[:, :].unsqueeze(1).to_broadcast([P, G, WIDE])
                            step = g * WIDES + b + done * WIDES
                            hot = v.scalar_tensor_tensor(wide, nodes, wstart[:, bass.ds(b, 1)], dst_g,
                                                         op0=ALU.add, op1=ALU.is_equal)
                            if weighted:
                                w = w_f[:, bass.ds(g * G, G)].unsqueeze(2).to_broadcast([P, G, WIDE])
                                hot.then_inc(wide_built, 1)
                                v.wait_ge(wide_built, g * WIDES + b + (weighted_done * WIDES + 1))
                                hot = v.tensor_tensor(wide, wide, w, ALU.mult)
                            hot.then_inc(wide_ready, 1)
                            nodes = acc[:, bass.ds(b * WIDE, WIDE)]
                            v.wait_ge(wide_summed, step + 1)
                            v.wait_ge(wide_added, step + 1)
                            v.tensor_tensor(nodes, nodes, pw[:, 0, :], ALU.add).then_inc(wide_added, 1)
                    v.wait_ge(wide_added, (done + GROUPS) * WIDES + 1)
                v.sem_inc(layer_summed, 1)

            def loop_chain(c, per_turn):
                base, k = steps[0], [0]
                steps[0] += per_turn * CHUNKS

                def then_(ins):
                    k[0] += 1
                    assert k[0] <= per_turn
                    ins.then_inc(dve_step, 1)
                    v.wait_ge(dve_step, c * per_turn + (base + k[0]))
                return then_

            def over_features(col):
                return col.unsqueeze(2).to_broadcast([P, CT, F])

            z = work[:, 0, :].rearrange("p (t f) -> p t f", f=F)
            e = work[:, 1, :].rearrange("p (t f) -> p t f", f=F)

            def normalise(c, n, then_):
                then_(v.tensor_reduce(mean, z, AX.X, ALU.add))
                then_(v.tensor_scalar(mean, mean, 1.0 / F, None, ALU.mult))
                v.tensor_tensor(z, z, over_features(mean), ALU.subtract).then_inc(y_ready, 1)
                v.wait_ge(sq_done, n + 1)
                then_(v.tensor_reduce(var, e, AX.X, ALU.add))
                v.tensor_scalar(var, var, 1.0 / F, EPS, ALU.mult, ALU.add).then_inc(v_ready, 1)
                v.wait_ge(sd_done, n + 1)
                then_(v.reciprocal(rstd, rstd))
                return v.tensor_tensor(xres[:, bass.ds(c * CT, CT), :], z, over_features(rstd), ALU.mult)

            aggregate(0)
            with v.Fori(0, CHUNKS) as c:
                v.tensor_scalar(hT[:, bass.ds(c * CN, CN)], acc[:, bass.ds(c * CN, CN)], 1.0, None, ALU.add)\
                 .then_inc(scaled, 1)
            with v.Fori(0, CHUNKS) as c:
                v.wait_ge(root_ready, c + 1)
                v.reciprocal(dis[:, bass.ds(c * CN, CN)], hT[:, bass.ds(c * CN, CN)]).then_inc(dis_ready, 1)
            v.wait_ge(dis_ready, CHUNKS)

            with v.Fori(0, CHUNKS) as c:
                v.wait_ge(a_full, c + 1)
                v.tensor_tensor(hT[:, bass.ds(c * CN, CN)].rearrange("p (t n) -> p t n", n=P), pa_t,
                                dis[:, bass.ds(c * CN, CN)].rearrange("p (t n) -> p t n", n=P), ALU.mult)\
                 .then_inc(h_ready, 1)
                v.wait_ge(h_ready, c + 1)
                v.sem_inc(a_free, 1)
            aggregate(1)

            for d in range(1, GCN_LAYERS):
                with v.Fori(0, CHUNKS) as c:
                    v.tensor_tensor(hT[:, bass.ds(c * CN, CN)], acc[:, bass.ds(c * CN, CN)],
                                    dis[:, bass.ds(c * CN, CN)], ALU.mult).then_inc(scaled, 1)
                with v.Fori(0, CHUNKS) as c:
                    v.wait_ge(relued, c + (CHUNKS * (d - 1) + 1))
                    v.tensor_tensor(hT[:, bass.ds(c * CN, CN)], hT[:, bass.ds(c * CN, CN)],
                                    dis[:, bass.ds(c * CN, CN)], ALU.mult).then_inc(h_ready, 1)
                aggregate(d + 1)

            with v.Fori(0, CHUNKS) as c:
                v.tensor_tensor(hT[:, bass.ds(c * CN, CN)], acc[:, bass.ds(c * CN, CN)],
                                dis[:, bass.ds(c * CN, CN)], ALU.mult).then_inc(scaled, 1)
            with v.Fori(0, CHUNKS) as c:
                then_ = loop_chain(c, 7)
                v.wait_ge(a_full, c * 2 + (CHUNKS + 1))
                then_(v.tensor_reduce(mx, pa_t, AX.X, ALU.max))
                v.tensor_tensor(z, pa_t, over_features(mx), ALU.subtract).then_inc(z_ready, 1)
                v.wait_ge(z_ready, c + 1)
                v.sem_inc(a_free, 1)
                v.wait_ge(exp_done, c + 1)
                v.tensor_reduce(ssum, e, AX.X, ALU.add).then_inc(s_ready, 1)
                then_(v.tensor_tensor(z, z, xres[:, bass.ds(c * CT, CT), :], ALU.add))
                v.wait_ge(ln_done, c + 1)
                then_(v.tensor_tensor(z, z, over_features(lnsum), ALU.subtract))
                normalise(c, c, then_).then_inc(x1_ready, 1)
                v.wait_ge(x1_ready, c + 1)
            aggregate(GCN_LAYERS + 1)
            aggregate(GCN_LAYERS + 2)

            with v.Fori(0, CHUNKS) as c:
                then_ = loop_chain(c, 4)
                v.wait_ge(a_full, c + (CHUNKS * 3 + 1))
                v.tensor_tensor(z, pa_t, xres[:, bass.ds(c * CT, CT), :], ALU.add).then_inc(z_ready, 1)
                v.wait_ge(z_ready, c + (CHUNKS + 1))
                v.sem_inc(a_free, 1)
                normalise(c, c + CHUNKS, then_).then_inc(out_ready, 1)
                v.wait_ge(out_ready, c + 1)

        @block.tensor
        def _(pe):
            pe.sem_inc(group_summed, U)
            pe.wait_ge(first_cast, 1)
            pe.matmul(pc[:, 0, 0:GROUPS], ones[0:1, :], first_f[0:1, :], start=True, stop=True)\
              .then_inc(first_spread, 1)
            pe.wait_ge(inwin_ready, 1)
            pe.matmul(pc[0:1, 1, 0:1], inwin[:, 0:1], ones[:, 0:1], start=True, stop=True)\
              .then_inc(inwin_summed, 1)
            pe.wait_ge(flag_ready, 1)
            slow = pe.value_load(slow_i[0:1, 0:1], min_val=0, max_val=N_EDGES)

            def aggregate(phase):
                done = GROUPS * phase
                ring = onehot_b if phase == 0 else onehot
                layer = phase - 1

                def rows_of(k):
                    return rows[:, k, :]

                def landed(i, k):
                    if phase > 0:
                        pe.wait_ge(row_landed[k], i * 16 + 16 * (TURNS * layer + 1))
                with pe.If(slow == 0):
                    with pe.Fori(0, TURNS) as i:
                        for u in range(U):
                            pe.wait_ge(window_added, i * U + (done + u + 1))
                            pe.wait_ge(onehot_ready, i * U + (done + u + 1))
                            for q in range(G):
                                k = u * G + q
                                landed(i, k)
                                mm = pe.matmul(window(u), ones_b[:, :] if phase == 0 else rows_of(k),
                                               ring[:, u, q, :], start=(q == 0), stop=(q == G - 1))
                            mm.then_inc(group_summed, 1)
                with pe.Else():
                    with pe.Fori(0, TURNS) as i:
                        for u in range(U):
                            for q in range(G):
                                landed(i, u * G + q)
                            pe.nop(nofuse=True)
                            with pe.Fori(0, WIDES) as b:
                                step = (i * U + (u + done)) * WIDES + b
                                pe.wait_ge(wide_added, step + 1)
                                pe.wait_ge(wide_ready, step + 1)
                                for q in range(G):
                                    mm = pe.matmul(pw[:, 0, :], ones[:, :] if phase == 0 else rows_of(u * G + q),
                                                   wide[:, q, :], start=(q == 0), stop=(q == G - 1))
                                mm.then_inc(wide_summed, 1)
                            pe.wait_ge(wide_summed, (i * U + (u + done + 1)) * WIDES)
                            pe.sem_inc(group_summed, 1)

            def transpose_chunk(n, tile_of, c):
                pe.wait_ge(a_free, n + 1)
                for j in range(CT):
                    t = pe.transpose(pa_t[:, j, :], tile_of(c, j), ident[:, :])
                t.then_inc(a_full, 1)

            def node_tile(c, j):
                return hT[:, bass.ds(c * CN + j * P, P)]

            def own_term(c, n, w):
                pe.wait_ge(c_free, n + 1)
                for a in range(2):
                    mm = pe.matmul(pc[:, a, 0:HALF], w, hT[:, bass.ds(c * CN + a * HALF, HALF)],
                                   start=True, stop=True)
                mm.then_inc(c_full, 1)

            def rel_rows_of(c, d):
                for j in range(CT):
                    pe.wait_ge(bt_free, c * CT + (NODE_TILES * d + j + (2 if j == 0 else 1)))
                    pe.matmul(pb[:, j % 2, :], node_tile(c, j), wr[:, d, :, :].rearrange("p r f -> p (r f)"),
                              start=True, stop=True).then_inc(bt_full, 1)

            aggregate(0)
            pe.wait_ge(loaded_x, 16)
            pe.wait_ge(loaded_w, 16 * 6)
            for d in range(GCN_LAYERS):
                for c in range(CHUNKS):
                    if d == 0:
                        transpose_chunk(c, lambda c, j: xres[:, bass.ds(c * CT + j, 1), :].rearrange("p a f -> p (a f)"), c)
                    pe.wait_ge(h_ready, c + (CHUNKS * d + 1))
                    pe.wait_ge(b_free, c + (CHUNKS * d + 1))
                    for j in range(CT):
                        mm = pe.matmul(pb_t[:, j, :], node_tile(c, j), wg[:, d, :], start=True, stop=True)
                    mm.then_inc(b_full, 1)
                    own_term(c, c + CHUNKS * d, wg[:, d, :])
                aggregate(d + 1)

            for c in range(CHUNKS):
                pe.wait_ge(relued, c + (CHUNKS * (GCN_LAYERS - 1) + 1))
                transpose_chunk(c * 2 + CHUNKS, node_tile, c)
                pe.wait_ge(x1_ready, c + 1)
                transpose_chunk(c * 2 + (CHUNKS + 1),
                                lambda c, j: xres[:, bass.ds(c * CT + j, 1), :].rearrange("p a f -> p (a f)"), c)
                pe.wait_ge(h_ready, c + (CHUNKS * GCN_LAYERS + 1))
                rel_rows_of(c, 0)
                own_term(c, c + CHUNKS * GCN_LAYERS, rr[:, 0, :])
            aggregate(GCN_LAYERS + 1)
            for c in range(CHUNKS):
                pe.wait_ge(h_ready, c + (CHUNKS * (GCN_LAYERS + 1) + 1))
                rel_rows_of(c, 1)
                own_term(c, c + CHUNKS * (GCN_LAYERS + 1), rr[:, 1, :])
            aggregate(GCN_LAYERS + 2)
            pe.wait_ge(layer_summed, PHASES)
            for c in range(CHUNKS):
                transpose_chunk(c + CHUNKS * 3, lambda c, j: acc[:, bass.ds(c * CN + j * P, P)], c)


def kernel(x, src, dst, edge_type_4, edge_weight, L0_gnn_W0, L0_gnn_W1, L0_gnn_W2, L0_gnn_b0, L0_gnn_b1, L0_gnn_b2,
           L1_gnn_W1, L1_gnn_root1, L1_gnn_b1, L1_gnn_W2, L1_gnn_root2, L1_gnn_b2):
    import numpy as np
    import concourse.bacc as bacc
    from concourse.bass_utils import run_bass_kernel_spmd

    def by_tile(a, pad):
        a = np.asarray(a)
        a = np.concatenate([a, np.full(TILES * P - N_EDGES, pad, a.dtype)])
        return np.ascontiguousarray(a.reshape(TILES, P).T)

    dst = np.asarray(dst)
    weight = np.asarray(edge_weight)
    firsts = np.concatenate([dst[::G * P], np.zeros(GROUPS, dst.dtype)])[:GROUPS]
    xp = np.concatenate([np.asarray(x), np.zeros((NODES - N_NODES, F), np.float32)])
    arrays = {
        "x": xp,
        "src": by_tile(src, 0),
        "dst": by_tile(dst, -1),
        "first_dst": np.ascontiguousarray(firsts[None, :]),
        "edge_type": by_tile(edge_type_4, 0),
        "weight": by_tile(weight, weight[-1]),
        "gcn_w": np.stack([np.asarray(w) for w in (L0_gnn_W0, L0_gnn_W1, L0_gnn_W2)]),
        "gcn_b": np.stack([np.asarray(b) for b in (L0_gnn_b0, L0_gnn_b1, L0_gnn_b2)], axis=1),
        "rel_w1": np.asarray(L1_gnn_W1),
        "rel_w2": np.asarray(L1_gnn_W2),
        "rel_root": np.stack([np.asarray(L1_gnn_root1), np.asarray(L1_gnn_root2)]),
        "rel_b": np.stack([np.asarray(L1_gnn_b1), np.asarray(L1_gnn_b2)], axis=1),
    }
    nc = bacc.Bacc("TRN2", target_bir_lowering=False, num_devices=1)
    args = {n: nc.dram_tensor(f"in_{n}", a.shape, mybir.dt.from_np(a.dtype), kind="ExternalInput").ap()
            for n, a in arrays.items()}
    out = nc.dram_tensor("out_0", (N_NODES, F), F32, kind="ExternalOutput").ap()
    build(nc, out=out, **args)
    r = run_bass_kernel_spmd(nc, [{f"in_{n}": a for n, a in arrays.items()}], core_ids=[0])
    return r.results[0]["out_0"]
```

```python
from contextlib import ExitStack

import concourse.bass as bass
from concourse import mybir

P = 128
N_NODES = 6250
N_EDGES = 106250
F = 128
R = 4
GCN_LAYERS = 3
REL_LAYERS = 2

NODE_TILES = -(-N_NODES // P)
NODES = NODE_TILES * P
CT = 7
CHUNKS = NODE_TILES // CT
CN = CT * P
HALF = CN // 2
LAST_ROWS = N_NODES - (NODE_TILES - 1) * P

G = 4
U = 4
SLOTS = G * U
TURNS = -(-N_EDGES // (P * SLOTS))
GROUPS = TURNS * U
TILES = TURNS * SLOTS
WIN = 64
WIDE = 512
WIDES = -(-NODES // WIDE)
ACC = WIDES * WIDE

DW = 8
DWINS = NODES // DW
DKEYS = DW * NODE_TILES
DE = 256
SKIP = 32
SKIP_ROWS = N_EDGES // SKIP + 1
GB = HALF
BLOCKS = NODES // GB
BW = GB // DW
QW = 4
QT = BW // QW
PIECE = 7
PIECES = NODE_TILES // PIECE

EPS = 1e-5

F32 = mybir.dt.float32
F16 = mybir.dt.float16
BF16 = mybir.dt.bfloat16
I32 = mybir.dt.int32
ALU = mybir.AluOpType
ACT = mybir.ActivationFunctionType
AX = mybir.AxisListType


class Ring:

    def __init__(self, sem, name, windows, gathers, weighted):
        self.group_summed = sem(name + "_group_summed")
        self.wide_ready = sem(name + "_wide_ready")
        self.wide_summed = sem(name + "_wide_summed")
        self.wide_added = sem(name + "_wide_added")
        if windows:
            self.onehot_ready = sem(name + "_onehot_ready")
            self.window_added = sem(name + "_window_added")
        if weighted:
            self.hot_built = sem(name + "_hot_built")
            self.wide_built = sem(name + "_wide_built")
        if gathers:
            self.idx_ready = sem(name + "_idx_ready")
            self.row_landed = [sem(f"{name}_row_landed{k}") for k in range(SLOTS)]
            self.term_ready = sem(name + "_term_ready")


def build(nc, x, src, dst, src_slots, dst_slots, first_dst, edge_type, weight, gcn_w, gcn_b, rel_w1, rel_w2,
          rel_root, rel_b, out):
    gcn_table = nc.dram_tensor("gcn_table", [NODES, F], F32, kind="Internal").ap()
    rel_table = nc.dram_tensor("rel_table", [NODES * R, F], F32, kind="Internal").ap()
    a_dram = nc.dram_tensor("a_dram", [BLOCKS, P, NODE_TILES * GB], F16, kind="Internal").ap()

    ctx = ExitStack()
    with ctx:
        def sb(name, shape, dt=F32):
            return ctx.enter_context(nc.sbuf_tensor(name, shape, dt))

        def sem(name):
            return ctx.enter_context(nc.semaphore(name))

        src_i = sb("src_i", [P, TILES], I32)
        rel_i = sb("rel_i", [P, TILES], I32)
        dst_f = sb("dst_f", [P, TILES])
        off_f = sb("off_f", [P, TILES])
        w_f = sb("w_f", [P, TILES])
        first_i = sb("first_i", [1, GROUPS], I32)
        big = sb("big", [P, NODE_TILES * GB])
        a_blocks = big[:, :].bitcast(F16).rearrange("p (s h n) -> p s h n", s=2, h=NODE_TILES)
        acc = big[:, 0:ACC]
        xres = big[:, ACC:ACC + NODES].rearrange("p (t f) -> p t f", f=F)
        tab = big[:, ACC + NODES:ACC + 2 * NODES]
        gcn_rows = tab.rearrange("p (t f) -> p t f", f=F)
        rel_rows = tab[:, 0:CT * R * F].rearrange("p (t f) -> p t f", f=R * F)
        nslot = CHUNKS * DE
        srcw = tab[:, 0:nslot].bitcast(I32)
        dstw = tab[:, nslot:2 * nslot].bitcast(I32)
        low = tab[:, 2 * nslot:3 * nslot]
        cnt_row = tab[0:1, 3 * nslot:3 * nslot + CN]
        hT = sb("hT", [P, NODES])
        type_i = hT[:, 0:TILES].bitcast(I32)
        wide = hT[:, 0:G * WIDE].rearrange("p (q n) -> p q n", q=G)
        dis = sb("dis", [P, NODES])
        g16 = sb("g16", [P, 2, NODE_TILES, F], F16)
        idx = sb("idx", [P, SLOTS], I32)
        rows_all = sb("rows", [P, SLOTS * F])
        rows = rows_all[:, :].rearrange("p (k f) -> p k f", f=F)
        low_t = rows_all[:, 0:2 * DWINS].rearrange("p (h w) -> p h w", h=2)
        low_hot = rows_all[:, 2 * DWINS:2 * DWINS + 2 * P].bitcast(F16).rearrange("p (w h n) -> p w h n", w=2, h=2)
        zeros16 = rows_all[:, SLOTS * F - GB // 2:SLOTS * F].bitcast(F16)
        hot_all = sb("onehot", [P, U * G * WIN])
        onehot = hot_all[:, :].rearrange("p (u q n) -> p u q n", u=U, q=G)
        onehot_b = hot_all[:, 0:U * G * WIN // 2].bitcast(BF16).rearrange("p (u q n) -> p u q n", u=U, q=G)
        key_hot = hot_all[:, 0:2 * DKEYS].bitcast(F16).rearrange("p (w h n) -> p w h n", w=2, h=2)
        work = sb("work", [P, 2 * CN])
        z_all, e_all = work[:, 0:CN], work[:, CN:2 * CN]
        iota_i = work[:, 0:WIDE].bitcast(I32)
        key_t = work[:, 0:2 * DWINS].rearrange("p (h w) -> p h w", h=2)
        iota = sb("iota", [P, WIDE])
        iota16 = sb("iota16", [P, DKEYS], F16)
        wstart = sb("wstart", [P, WIDES])
        w8_i = sb("w8_i", [P, CHUNKS], I32)
        ident = sb("ident", [P, P])
        ident16 = sb("ident16", [P, P], F16)
        before = sb("before", [P, P])
        ones = sb("ones", [P, P])
        ones_b = sb("ones_b", [P, P], BF16)
        wg = sb("wg", [P, GCN_LAYERS, F])
        bg = sb("bg", [P, GCN_LAYERS])
        wr = sb("wr", [P, REL_LAYERS, R, F])
        rr = sb("rr", [P, REL_LAYERS, F])
        br = sb("br", [P, REL_LAYERS])
        small = sb("small", [P, 6, 8])
        mx, ssum, lnsum, mean, var, rstd = (small[:, k, 0:CT] for k in range(6))
        tiny = sb("tiny", [P, 64])
        ext, ext_all = tiny[:, 0:2], tiny[:, 2:4]
        span = tiny[:, 4:8]
        inwin = tiny[:, 8:10]
        cnt, pre = tiny[:, 10:17], tiny[:, 17:24]
        gmax = tiny[:, 24:31]
        gtop, gtop_all = tiny[:, 31:32], tiny[:, 32:33]
        power, scale, unscale = tiny[:, 33:34], tiny[:, 34:35], tiny[:, 35:36]
        block_i = sb("block_i", [P, 8], I32)
        slow_i = sb("slow_i", [1, 2], I32)

        pa = ctx.enter_context(nc.psum_tensor("pa", [P, 2, 512], F32))
        pb = ctx.enter_context(nc.psum_tensor("pb", [P, 2, 512], F32))
        pc = ctx.enter_context(nc.psum_tensor("pc", [P, 2, 512], F32))
        pw = ctx.enter_context(nc.psum_tensor("pw", [P, 2, 512], F32))

        def tiles_of(bank):
            return bank[:, :, :].rearrange("p a n -> p (a n)")[:, 0:CN].rearrange("p (t f) -> p t f", f=F)
        pa_t, pb_t, pw_t = tiles_of(pa), tiles_of(pb), tiles_of(pw)

        def window(u):
            return (pw if u < 2 else pb)[:, u % 2, 0:WIN]

        deg = Ring(sem, "deg", windows=True, gathers=False, weighted=False)
        gcn = Ring(sem, "gcn", windows=False, gathers=True, weighted=False)
        rel = Ring(sem, "rel", windows=True, gathers=True, weighted=True)
        summed_all = sem("summed_all")
        loaded_edges = sem("loaded_edges")
        loaded_x = sem("loaded_x")
        loaded_w = sem("loaded_w")
        consts_made = sem("consts_made")
        dve_step = sem("dve_step")
        ones_ready = sem("ones_ready")
        ext_ready = sem("ext_ready")
        ext_reduced = sem("ext_reduced")
        first_spread = sem("first_spread")
        inwin_ready = sem("inwin_ready")
        inwin_summed = sem("inwin_summed")
        flag_ready = sem("flag_ready")
        degree_ready = sem("degree_ready")
        root_ready = sem("root_ready")
        dis_ready = sem("dis_ready")
        cnt_ready = sem("cnt_ready")
        cnt_spread = sem("cnt_spread")
        pre_ready = sem("pre_ready")
        start_ready = sem("start_ready")
        block_ready = sem("block_ready")
        slots_landed = sem("slots_landed")
        keys_ready = sem("keys_ready")
        key_turned = sem("key_turned")
        key_kept = sem("key_kept")
        a_full = sem("a_full")
        a_free = sem("a_free")
        x_scaled = sem("x_scaled")
        hots_ready = sem("hots_ready")
        window_built = sem("window_built")
        pair_kept = sem("pair_kept")
        block_stored = sem("block_stored")
        block_safe = sem("block_safe")
        piece_landed = gcn.row_landed[0:2 * PIECES]
        piece_used = sem("piece_used")
        g_full = sem("g_full")
        g_seen = sem("g_seen")
        top_ready = sem("top_ready")
        top_reduced = sem("top_reduced")
        scale_ready = sem("scale_ready")
        high_ready = sem("high_ready")
        low_ready = sem("low_ready")
        block_summed = sem("block_summed")
        block_scaled = sem("block_scaled")
        block_relued = sem("block_relued")
        block_next = sem("block_next")
        scaled = sem("scaled")
        relued = sem("relued")
        h_ready = sem("h_ready")
        b_full = sem("b_full")
        b_free = sem("b_free")
        c_full = sem("c_full")
        c_free = sem("c_free")
        rows_filled = sem("rows_filled")
        rows_stored = sem("rows_stored")
        h3_ready = sem("h3_ready")
        x_back = sem("x_back")
        in_ready = sem("in_ready")
        bt_full = sem("bt_full")
        bt_free = sem("bt_free")
        cr_full = sem("cr_full")
        cr_free = sem("cr_free")
        rel_filled = sem("rel_filled")
        rel_stored = [sem(f"rel_stored{j}") for j in range(CT)]
        rel_free = sem("rel_free")
        z_ready = sem("z_ready")
        exp_done = sem("exp_done")
        s_ready = sem("s_ready")
        ln_done = sem("ln_done")
        y_ready = sem("y_ready")
        sq_done = sem("sq_done")
        v_ready = sem("v_ready")
        sd_done = sem("sd_done")
        x1_ready = sem("x1_ready")
        out_ready = sem("out_ready")
        out_stored = sem("out_stored")

        def flag(eng, which):
            eng.wait_ge(flag_ready, which + 1)
            return eng.value_load(slow_i[0:1, which:which + 1], min_val=0, max_val=N_EDGES)

        block = ctx.enter_context(nc.Block())

        @block.sync
        def _(sp):
            sp.sem_inc(rel_free, CT)
            sp.sem_inc(block_safe, 2)
            for tile_, arr in ((dst_f[:, :].bitcast(I32), dst), (w_f[:, :], weight)):
                sp.dma_start(tile_, arr).then_inc(loaded_edges, 16)
            sp.dma_start(first_i[:, :], first_dst).then_inc(loaded_edges, 16)
            sp.dma_start(src_i[:, :], src).then_inc(loaded_edges, 16)
            sp.dma_start(type_i, edge_type).then_inc(loaded_edges, 16)
            sp.dma_start(xres, x.rearrange("(t p) f -> p t f", p=P)).then_inc(loaded_x, 16)
            sp.dma_start(wg[:, :, :], gcn_w.rearrange("l i o -> i l o")).then_inc(loaded_w, 16)
            sp.dma_start(bg[:, :], gcn_b).then_inc(loaded_w, 16)
            sp.dma_start(wr[:, 0, :, :], rel_w1.rearrange("r i o -> i r o")).then_inc(loaded_w, 16)
            sp.dma_start(wr[:, 1, :, :], rel_w2.rearrange("r i o -> i r o")).then_inc(loaded_w, 16)
            sp.dma_start(rr[:, :, :], rel_root.rearrange("l i o -> i l o")).then_inc(loaded_w, 16)
            sp.dma_start(br[:, :], rel_b).then_inc(loaded_w, 16)

            slow = flag(sp, 1)
            with sp.If(slow == 0):
                with sp.Fori(0, BLOCKS // 2) as c:
                    for s in range(2):
                        b = c * 2 + s
                        sp.wait_ge(pair_kept, b * (BW // 2) + (2 + BW // 2))
                        sp.dma_start(a_dram[bass.ds(b, 1)].rearrange("a p n -> (a p) n"),
                                     a_blocks[:, s].rearrange("p h n -> p (h n)")).then_inc(block_stored, 16)
                        sp.wait_ge(block_stored, b * 16 + 16)
                        sp.sem_inc(block_safe, 1)
                sp.wait_ge(block_summed, 2 + BLOCKS)
                for layer in range(1, GCN_LAYERS):
                    with sp.Fori(0, BLOCKS // 2) as c:
                        for s in range(2):
                            for k in range(PIECES):
                                n = c * (2 * PIECES) + ((layer - 1) * BLOCKS * PIECES + s * PIECES + k)
                                sp.wait_ge(piece_used, n + 1)
                                sp.dma_start(
                                    a_blocks[:, s, k * PIECE:(k + 1) * PIECE, :].rearrange("p h n -> p (h n)"),
                                    a_dram[bass.ds(c * 2 + s, 1), :, k * PIECE * GB:(k + 1) * PIECE * GB]
                                    .rearrange("a p n -> (a p) n"),
                                ).then_inc(piece_landed[s * PIECES + k], 16)
            with sp.Else():
                gcn_out = gcn_table.rearrange("(c t p) f -> c p t f", p=P, t=CT)
                for d in range(GCN_LAYERS):
                    with sp.Fori(0, CHUNKS) as c:
                        sp.wait_ge(rows_filled, c + (CHUNKS * d + 1))
                        sp.dma_start(gcn_out[bass.ds(c, 1)].rearrange("a p t f -> p (a t) f"),
                                     gcn_rows[:, bass.ds(c * CT, CT), :]).then_inc(rows_stored, 16)
                sp.wait_ge(rows_stored, 16 * CHUNKS * GCN_LAYERS)

            sp.wait_ge(h3_ready, 1)
            sp.dma_start(xres, x.rearrange("(t p) f -> p t f", p=P)).then_inc(x_back, 16)
            rel_out = rel_table.rearrange("(c t p r) f -> (c t) p (r f)", p=P, t=CT, r=R)
            for d in range(REL_LAYERS):
                with sp.Fori(0, CHUNKS) as c:
                    for j in range(CT):
                        sp.wait_ge(rel_filled, c * CT + (NODE_TILES * d + j + 1))
                        sp.dma_start(rel_out[bass.ds(c * CT + j, 1)].rearrange("a p f -> (a p) f"),
                                     rel_rows[:, j, :]).then_inc(rel_stored[j], 16)
                    for j in range(CT):
                        sp.wait_ge(rel_stored[j], c * 16 + 16 * (CHUNKS * d + 1))
                        sp.sem_inc(rel_free, 1)
            out_v = out[0:(NODE_TILES - 1) * P, :].rearrange("(t p) f -> p t f", p=P)
            with sp.Fori(0, CHUNKS - 1) as c:
                sp.wait_ge(out_ready, c + 1)
                sp.dma_start(out_v[:, bass.ds(c * CT, CT), :], xres[:, bass.ds(c * CT, CT), :])\
                  .then_inc(out_stored, 16)
            sp.wait_ge(out_ready, CHUNKS)
            t0 = (CHUNKS - 1) * CT
            sp.dma_start(out_v[:, t0:NODE_TILES - 1, :], xres[:, t0:NODE_TILES - 1, :]).then_inc(out_stored, 16)
            sp.dma_start(out[(NODE_TILES - 1) * P:N_NODES, :], xres[0:LAST_ROWS, NODE_TILES - 1, :])\
              .then_inc(out_stored, 16)
            sp.wait_ge(out_stored, 16 * (CHUNKS + 1))

        @block.gpsimd
        def _(pool):
            pool.iota(iota_i, pattern=[[1, WIDE]], base=0, channel_multiplier=0).then_inc(consts_made, 1)
            pool.iota(w8_i[:, :], pattern=[[P * DW, CHUNKS]], base=0, channel_multiplier=DW).then_inc(consts_made, 1)
            pool.memset(ident[:, :], 0.0).then_inc(consts_made, 1)
            pool.memset(before[:, :], 1.0).then_inc(consts_made, 1)
            pool.wait_ge(consts_made, 4)
            pool.affine_select(out=ident[:, :], in_=ident[:, :], compare_op=ALU.not_equal, fill=1.0,
                               base=0, pattern=[[-1, P]], channel_multiplier=1).then_inc(consts_made, 1)
            pool.affine_select(out=before[:, :], in_=before[:, :], compare_op=ALU.is_gt, fill=0.0,
                               base=0, pattern=[[1, P]], channel_multiplier=-1).then_inc(consts_made, 1)
            pool.wait_ge(ext_ready, 1)
            pool.partition_all_reduce(ext_all, ext, P, bass.bass_isa.ReduceOp.max).then_inc(ext_reduced, 1)

            pool.wait_ge(block_ready, 1)
            for c in range(CHUNKS):
                for slots, table in ((srcw, src_slots), (dstw, dst_slots)):
                    pool.indirect_dma_start(
                        out=slots[:, c * DE:(c + 1) * DE], out_offset=None, in_=table,
                        in_offset=bass.IndirectOffsetOnAxis(ap=block_i[:, c:c + 1], axis=0),
                    ).then_inc(slots_landed, 16)

            def gather(table, ring, n):
                with pool.Fori(0, TURNS) as i:
                    for k in range(SLOTS):
                        if k % (SLOTS // 2) == 0:
                            pool.wait_ge(ring.idx_ready, i * 2 + (2 * TURNS * n + k // (SLOTS // 2) + 1))
                        if k % G == 0:
                            pool.wait_ge(ring.group_summed, i * U + (GROUPS * n + k // G + 1))
                            pool.nop(nofuse=True)
                        pool.indirect_dma_start(
                            out=rows[:, k, :], out_offset=None, in_=table,
                            in_offset=bass.IndirectOffsetOnAxis(ap=idx[:, k:k + 1], axis=0),
                        ).then_inc(ring.row_landed[k], 16)

            slow = flag(pool, 1)
            with pool.If(slow == 0):
                for layer in range(GCN_LAYERS):
                    pool.wait_ge(top_ready, layer + 1)
                    pool.partition_all_reduce(gtop_all, gtop, P, bass.bass_isa.ReduceOp.max)\
                        .then_inc(top_reduced, 1)
                    if layer < GCN_LAYERS - 1:
                        with pool.Fori(0, BLOCKS) as b:
                            nodes = bass.ds(b * GB, GB)
                            pool.wait_ge(block_relued, b + (BLOCKS * layer + 1))
                            pool.tensor_tensor(hT[:, nodes], hT[:, nodes], dis[:, nodes], ALU.mult)\
                                .then_inc(block_next, 1)
            with pool.Else():
                for layer in range(GCN_LAYERS):
                    pool.wait_ge(rows_stored, 16 * CHUNKS * (layer + 1))
                    gather(gcn_table, gcn, layer)
            for d in range(REL_LAYERS):
                pool.wait_ge(rel_free, CT + NODE_TILES * (d + 1))
                gather(rel_table, rel, d)

        @block.scalar
        def _(act):
            act.sem_inc(pair_kept, 2)
            act.sem_inc(b_free, 1)
            act.sem_inc(bt_free, 2)
            act.sem_inc(c_free, 1)
            act.sem_inc(cr_free, 1)
            act.wait_ge(loaded_edges, 16 * 5)
            act.wait_ge(loaded_w, 16 * 6)

            def activation(out_, in_, func, **kw):
                act.nop(nofuse=True)
                return act.activation(out_, in_, func, **kw)

            with act.Fori(0, CHUNKS) as c:
                act.wait_ge(degree_ready, c + 1)
                activation(hT[:, bass.ds(c * CN, CN)], hT[:, bass.ds(c * CN, CN)], ACT.Sqrt)\
                    .then_inc(root_ready, 1)

            def copy_indices(table_rows, ring, n):
                half = SLOTS // 2
                with act.Fori(0, TURNS) as i:
                    for h in range(2):
                        act.wait_ge(ring.group_summed, i * U + (GROUPS * n + (h + 1) * U // 2))
                        activation(idx[:, h * half:(h + 1) * half],
                                   table_rows[:, bass.ds(i * SLOTS + h * half, half)], ACT.Copy)\
                            .then_inc(ring.idx_ready, 1)

            def own_term(c, n, ring, full, free, bias):
                act.wait_ge(full, n + 1)
                nodes = acc[:, bass.ds(c * CN, CN)].rearrange("p (a n) -> p a n", a=2)
                if bias is None:
                    activation(nodes, pc[:, :, 0:HALF], ACT.Copy).then_inc(ring.term_ready, 1)
                else:
                    activation(nodes, pc[:, :, 0:HALF], ACT.Identity, bias=bias).then_inc(ring.term_ready, 1)
                act.wait_ge(ring.term_ready, n + 1)
                act.sem_inc(free, 1)

            def keep_block(b, s):
                act.wait_ge(block_summed, b + 1)
                act.wait_ge(block_safe, b + 1)
                with act.Fori(0, QT) as q:
                    for k, bank in enumerate((pw, pb)):
                        act.wait_ge(window_built, (b * BW + q * QW) + (2 + 2 * k + 2))
                        at = a_blocks[:, s, :, bass.ds(q * (QW * DW) + k * 2 * DW, 2 * DW)]
                        activation(at.rearrange("p h (w d) -> p w h d", w=2),
                                   bank[:, :, 0:DKEYS].rearrange("p w (d h) -> p w h d", d=DW), ACT.Copy)\
                            .then_inc(pair_kept, 1)

            def relu_block(b, layer):
                nodes = bass.ds(b * GB, GB)
                act.wait_ge(block_scaled, b + (BLOCKS * layer + 3))
                activation(hT[:, nodes], hT[:, nodes], ACT.Relu, bias=bg[:, layer:layer + 1])\
                    .then_inc(block_relued, 1)

            slow = flag(act, 1)
            with act.If(slow == 0):
                for layer in range(GCN_LAYERS):
                    act.wait_ge(scale_ready, layer + 1)
                    for c in range(CHUNKS):
                        act.wait_ge(g_full, 2 * CHUNKS * layer + CHUNKS + c + 1)
                        activation(g16[:, 0, c * CT:(c + 1) * CT, :], pw_t if c % 2 else pb_t, ACT.Identity,
                                   scale=scale).then_inc(high_ready, 1)
                    if layer == 0:
                        keep_block(0, 0)
                        with act.Fori(0, BLOCKS // 2 - 1) as c:
                            for s in range(2):
                                keep_block(c * 2 + (s + 1), 1 - s)
                                relu_block(c * 2 + s, 0)
                        keep_block(BLOCKS - 1, 1)
                        relu_block(BLOCKS - 2, 0)
                        relu_block(BLOCKS - 1, 0)
                    else:
                        with act.Fori(0, BLOCKS) as b:
                            relu_block(b, layer)
                act.wait_ge(block_relued, BLOCKS * GCN_LAYERS)
            with act.Else():
                for d in range(GCN_LAYERS):
                    with act.Fori(0, CHUNKS) as c:
                        chunk = hT[:, bass.ds(c * CN, CN)]
                        if d > 0:
                            act.wait_ge(scaled, c + (CHUNKS * (d - 1) + 1))
                            activation(chunk, chunk, ACT.Relu, bias=bg[:, d - 1:d]).then_inc(relued, 1)
                        act.wait_ge(b_full, c + (CHUNKS * d + 1))
                        activation(gcn_rows[:, bass.ds(c * CT, CT), :], pb_t, ACT.Copy).then_inc(rows_filled, 1)
                        act.wait_ge(rows_filled, c + (CHUNKS * d + 1))
                        act.sem_inc(b_free, 1)
                        own_term(c, c + CHUNKS * d, gcn, c_full, c_free, None)
                    copy_indices(src_i, gcn, d)
                with act.Fori(0, CHUNKS) as c:
                    chunk = hT[:, bass.ds(c * CN, CN)]
                    act.wait_ge(scaled, c + (CHUNKS * (GCN_LAYERS - 1) + 1))
                    activation(chunk, chunk, ACT.Relu, bias=bg[:, GCN_LAYERS - 1:GCN_LAYERS]).then_inc(relued, 1)
                act.wait_ge(relued, CHUNKS * GCN_LAYERS)
            act.sem_inc(h3_ready, 1)

            def rel_rows_out(c, d):
                for j in range(CT):
                    act.wait_ge(bt_full, c * CT + (NODE_TILES * d + j + 1))
                    act.wait_ge(rel_free, c * CT + (NODE_TILES * d + j + 1))
                    activation(rel_rows[:, j, :], pb[:, j % 2, :], ACT.Copy).then_inc(rel_filled, 1)
                    act.wait_ge(rel_filled, c * CT + (NODE_TILES * d + j + 1))
                    act.sem_inc(bt_free, 1)

            with act.Fori(0, CHUNKS) as c:
                chunk = hT[:, bass.ds(c * CN, CN)]
                act.wait_ge(z_ready, c + 1)
                activation(e_all, z_all, ACT.Exp).then_inc(exp_done, 1)
                act.wait_ge(s_ready, c + 1)
                activation(lnsum, ssum, ACT.Ln).then_inc(ln_done, 1)
                act.wait_ge(y_ready, c + 1)
                activation(e_all, z_all, ACT.Square).then_inc(sq_done, 1)
                act.wait_ge(v_ready, c + 1)
                activation(rstd, var, ACT.Sqrt).then_inc(sd_done, 1)
                act.wait_ge(a_full, c * 2 + (CHUNKS + 2))
                activation(chunk.rearrange("p (t n) -> p t n", n=P), pa_t, ACT.Copy).then_inc(in_ready, 1)
                act.wait_ge(in_ready, c + 1)
                act.sem_inc(a_free, 1)
                rel_rows_out(c, 0)
                own_term(c, c, rel, cr_full, cr_free, br[:, 0:1])
            copy_indices(rel_i, rel, 0)

            act.wait_ge(summed_all, 1)
            with act.Fori(0, CHUNKS) as c:
                activation(hT[:, bass.ds(c * CN, CN)], acc[:, bass.ds(c * CN, CN)], ACT.Relu)\
                    .then_inc(in_ready, 1)
                rel_rows_out(c, 1)
                own_term(c, c + CHUNKS, rel, cr_full, cr_free, br[:, 1:2])
            copy_indices(rel_i, rel, 1)

            with act.Fori(0, CHUNKS) as c:
                act.wait_ge(y_ready, c + (CHUNKS + 1))
                activation(e_all, z_all, ACT.Square).then_inc(sq_done, 1)
                act.wait_ge(v_ready, c + (CHUNKS + 1))
                activation(rstd, var, ACT.Sqrt).then_inc(sd_done, 1)

        @block.vector
        def _(v):
            steps = [0]

            def then(ins):
                steps[0] += 1
                ins.then_inc(dve_step, 1)
                v.wait_ge(dve_step, steps[0])

            v.sem_inc(a_free, 1)
            v.sem_inc(block_scaled, 2)
            for ring in (deg, gcn, rel):
                if ring is not gcn:
                    v.sem_inc(ring.window_added, U)
                v.sem_inc(ring.wide_added, 1)
            v.memset(ones[:, :], 1.0).then_inc(ones_ready, 1)
            v.memset(ones_b[:, :], 1.0).then_inc(ones_ready, 1)
            then(v.memset(zeros16, 0.0))
            then(v.memset(acc, 0.0))
            then(v.memset(cnt_row, 0.0))
            v.wait_ge(consts_made, 6)
            then(v.tensor_copy(iota[:, :], iota_i))
            then(v.tensor_copy(iota16[:, :], iota[:, 0:DKEYS]))
            then(v.tensor_copy(ident16[:, :], ident[:, :]))
            then(v.tensor_scalar(wstart[:, :], iota_i[:, 0:WIDES], float(WIDE), None, ALU.mult))

            v.wait_ge(loaded_edges, 16 * 5)
            first_f = e_all[0:1, 0:GROUPS]
            then(v.tensor_copy(first_f, first_i[:, :]))
            v.sem_inc(ones_ready, 1)
            then(v.tensor_copy(off_f[:, :], dst_f[:, :].bitcast(I32)))
            then(v.tensor_copy(dst_f[:, :], off_f[:, :]))

            then(v.tensor_copy(off_f[:, :], src_i[:, :]))
            then(v.tensor_copy(z_all[:, 0:TILES], type_i))
            then(v.scalar_tensor_tensor(rel_i[:, :], off_f[:, :], float(R), z_all[:, 0:TILES],
                                        op0=ALU.mult, op1=ALU.add))
            then(v.tensor_reduce(ext[:, 0:1], w_f[:, :], AX.X, ALU.min))
            then(v.tensor_scalar(ext[:, 0:1], ext[:, 0:1], -1.0, None, ALU.mult))
            v.tensor_reduce(ext[:, 1:2], w_f[:, :], AX.X, ALU.max).then_inc(ext_ready, 1)
            v.wait_ge(ext_reduced, 1)
            then(v.tensor_tensor(span[:, 0:1], ext_all[:, 0:1], ext_all[:, 1:2], ALU.add))
            then(v.tensor_scalar(span[:, 1:2], span[:, 0:1], 1e-8, None, ALU.add))
            then(v.reciprocal(span[:, 2:3], span[:, 1:2]))
            then(v.tensor_scalar(w_f[:, :], w_f[:, :], ext_all[:, 0:1], span[:, 2:3], ALU.add, ALU.mult))

            v.wait_ge(first_spread, 1)
            then(v.tensor_copy(e_all[:, 0:GROUPS], pc[:, 0, 0:GROUPS]))
            then(v.tensor_tensor(off_f[:, :].rearrange("p (g k) -> p g k", k=G),
                                 dst_f[:, :].rearrange("p (g k) -> p g k", k=G),
                                 e_all[:, 0:GROUPS].unsqueeze(2).to_broadcast([P, GROUPS, G]), ALU.subtract))
            then(v.tensor_scalar(z_all[:, 0:TILES], off_f[:, :], 0.0, None, ALU.is_ge))
            then(v.scalar_tensor_tensor(z_all[:, 0:TILES], off_f[:, :], float(WIN), z_all[:, 0:TILES],
                                        op0=ALU.is_lt, op1=ALU.mult))
            v.tensor_reduce(inwin[:, 0:1], z_all[:, 0:TILES], AX.X, ALU.add).then_inc(inwin_ready, 1)
            v.wait_ge(inwin_summed, 1)
            v.tensor_scalar(slow_i[0:1, 0:1], pc[0:1, 1, 0:1], -1.0, float(N_EDGES), ALU.mult, ALU.add)\
             .then_inc(flag_ready, 1)
            sparse_slow = flag(v, 0)

            def hots_of(ring, hots, n, weighted, i, u):
                off = off_f[:, bass.ds(i * SLOTS + u * G, G)].unsqueeze(2).to_broadcast([P, G, WIN])
                nodes = iota[:, 0:WIN].unsqueeze(1).to_broadcast([P, G, WIN])
                v.wait_ge(ring.group_summed, i * U + (GROUPS * n + u + 1))
                if weighted:
                    w = w_f[:, bass.ds(i * SLOTS + u * G, G)].unsqueeze(2).to_broadcast([P, G, WIN])
                    v.tensor_tensor(hots[:, u], off, nodes, ALU.is_equal).then_inc(ring.hot_built, 1)
                    v.wait_ge(ring.hot_built, i * U + (GROUPS * n + u + 1))
                    v.tensor_tensor(hots[:, u], hots[:, u], w, ALU.mult).then_inc(ring.onehot_ready, 1)
                else:
                    v.tensor_tensor(hots[:, u], off, nodes, ALU.is_equal).then_inc(ring.onehot_ready, 1)

            def load_firsts(i):
                return [v.value_load(first_i[0:1, bass.ds(i * U + u, 1)], min_val=0, max_val=N_NODES - 1)
                        for u in range(U)]

            def add_window(ring, n, first, i, u):
                nodes = acc[:, bass.ds(first, WIN)]
                v.wait_ge(ring.group_summed, i * U + (GROUPS * n + U + u + 1))
                v.wait_ge(ring.window_added, i * U + (GROUPS * n + U + u))
                v.tensor_tensor(nodes, nodes, window(u), ALU.add).then_inc(ring.window_added, 1)

            def aggregate_windows(ring, n, weighted):
                hots = onehot_b if ring is deg else onehot
                for u in range(U):
                    hots_of(ring, hots, n, weighted, 0, u)
                with v.Fori(1, TURNS) as i:
                    firsts = load_firsts(i - 1)
                    for u in range(U):
                        hots_of(ring, hots, n, weighted, i, u)
                        add_window(ring, n, firsts[u], i - 1, u)
                firsts = load_firsts(TURNS - 1)
                for u in range(U):
                    add_window(ring, n, firsts[u], TURNS - 1, u)
                v.wait_ge(ring.window_added, GROUPS * (n + 1) + U)

            def aggregate_wide(ring, n, weighted):
                done = GROUPS * n
                with v.Fori(0, GROUPS) as g:
                    with v.Fori(0, WIDES) as b:
                        dst_g = dst_f[:, bass.ds(g * G, G)].unsqueeze(2).to_broadcast([P, G, WIDE])
                        nodes = iota[:, :].unsqueeze(1).to_broadcast([P, G, WIDE])
                        step = g * WIDES + b + done * WIDES
                        hot = v.scalar_tensor_tensor(wide, nodes, wstart[:, bass.ds(b, 1)], dst_g,
                                                     op0=ALU.add, op1=ALU.is_equal)
                        if weighted:
                            w = w_f[:, bass.ds(g * G, G)].unsqueeze(2).to_broadcast([P, G, WIDE])
                            hot.then_inc(ring.wide_built, 1)
                            v.wait_ge(ring.wide_built, step + 1)
                            hot = v.tensor_tensor(wide, wide, w, ALU.mult)
                        hot.then_inc(ring.wide_ready, 1)
                        nodes = acc[:, bass.ds(b * WIDE, WIDE)]
                        v.wait_ge(ring.wide_summed, step + 1)
                        v.wait_ge(ring.wide_added, step + 1)
                        v.tensor_tensor(nodes, nodes, pw[:, 0, :], ALU.add).then_inc(ring.wide_added, 1)
                v.wait_ge(ring.wide_added, (done + GROUPS) * WIDES + 1)

            def loop_chain(c, per_turn):
                base, k = steps[0], [0]
                steps[0] += per_turn * CHUNKS

                def then_(ins):
                    k[0] += 1
                    assert k[0] <= per_turn
                    ins.then_inc(dve_step, 1)
                    v.wait_ge(dve_step, c * per_turn + (base + k[0]))
                return then_

            def over_features(col):
                return col.unsqueeze(2).to_broadcast([P, CT, F])

            z = z_all.rearrange("p (t f) -> p t f", f=F)
            e = e_all.rearrange("p (t f) -> p t f", f=F)

            def normalise(c, n, then_):
                then_(v.tensor_reduce(mean, z, AX.X, ALU.add))
                then_(v.tensor_scalar(mean, mean, 1.0 / F, None, ALU.mult))
                v.tensor_tensor(z, z, over_features(mean), ALU.subtract).then_inc(y_ready, 1)
                v.wait_ge(sq_done, n + 1)
                then_(v.tensor_reduce(var, e, AX.X, ALU.add))
                v.tensor_scalar(var, var, 1.0 / F, EPS, ALU.mult, ALU.add).then_inc(v_ready, 1)
                v.wait_ge(sd_done, n + 1)
                then_(v.reciprocal(rstd, rstd))
                return v.tensor_tensor(xres[:, bass.ds(c * CT, CT), :], z, over_features(rstd), ALU.mult)

            with v.If(sparse_slow == 0):
                aggregate_windows(deg, 0, False)
            with v.Else():
                aggregate_wide(deg, 0, False)
            v.tensor_reduce(cnt_row[:, 0:DWINS], acc[0:1, 0:NODES].rearrange("p (w d) -> p w d", d=DW), AX.X, ALU.add)\
             .then_inc(cnt_ready, 1)
            with v.Fori(0, CHUNKS) as c:
                v.tensor_scalar(hT[:, bass.ds(c * CN, CN)], acc[:, bass.ds(c * CN, CN)], 1.0, None, ALU.add)\
                 .then_inc(degree_ready, 1)
            v.wait_ge(cnt_spread, 1)
            then(v.tensor_copy(cnt, pc[:, 0, 0:CHUNKS]))
            then(v.memset(pre[:, 0:1], 0.0))
            for c in range(1, CHUNKS):
                then(v.tensor_tensor(pre[:, c:c + 1], pre[:, c - 1:c], cnt[:, c - 1:c], ALU.add))
            v.sem_inc(pre_ready, 1)
            v.wait_ge(start_ready, 1)
            then(v.tensor_copy(block_i[:, 0:CHUNKS], pc[:, 1, 0:CHUNKS]))
            v.tensor_scalar(block_i[:, 0:CHUNKS], block_i[:, 0:CHUNKS], SKIP.bit_length() - 1, None,
                            ALU.logical_shift_right).then_inc(block_ready, 1)
            with v.Fori(0, CHUNKS) as c:
                v.wait_ge(root_ready, c + 1)
                v.reciprocal(dis[:, bass.ds(c * CN, CN)], hT[:, bass.ds(c * CN, CN)]).then_inc(dis_ready, 1)
            v.wait_ge(dis_ready, CHUNKS)
            with v.Fori(0, CHUNKS) as c:
                v.wait_ge(a_full, c + 1)
                v.tensor_tensor(hT[:, bass.ds(c * CN, CN)].rearrange("p (t n) -> p t n", n=P), pa_t,
                                dis[:, bass.ds(c * CN, CN)].rearrange("p (t n) -> p t n", n=P), ALU.mult)\
                 .then_inc(x_scaled, 1)
                v.wait_ge(x_scaled, c + 1)
                v.sem_inc(a_free, 1)

            v.wait_ge(slots_landed, 16 * 2 * CHUNKS)
            key = dstw.bitcast(F32)
            scratch = work[:, 0:nslot]
            then(v.tensor_scalar(scratch.bitcast(I32), srcw, P - 1, None, ALU.bitwise_and))
            then(v.tensor_copy(low, scratch.bitcast(I32)))
            then(v.tensor_scalar(srcw, srcw, P.bit_length() - 1, None, ALU.logical_shift_right))
            then(v.tensor_tensor(key.rearrange("p (c e) -> p c e", c=CHUNKS), dstw.rearrange("p (c e) -> p c e", c=CHUNKS),
                                 w8_i[:, :].unsqueeze(2).to_broadcast([P, CHUNKS, DE]), ALU.subtract))
            then(v.scalar_tensor_tensor(key, key, float(NODE_TILES), srcw, op0=ALU.mult, op1=ALU.add))
            then(v.tensor_scalar(scratch, key, 0.0, None, ALU.is_ge))
            v.sem_inc(keys_ready, 1)
            then(v.scalar_tensor_tensor(scratch, key, float(DKEYS), scratch, op0=ALU.is_lt, op1=ALU.mult))
            v.tensor_reduce(inwin[:, 1:2], scratch, AX.X, ALU.add).then_inc(inwin_ready, 1)
            v.wait_ge(inwin_summed, 2)
            v.tensor_scalar(slow_i[0:1, 1:2], pc[0:1, 1, 0:1], -1.0, float(N_EDGES), ALU.mult, ALU.add)\
             .then_inc(flag_ready, 1)
            for c in range(CHUNKS):
                n = min(P, DWINS - c * P)
                v.wait_ge(key_turned, c + 1)
                both = pa[:, c % 2, :].rearrange("p (m h w) -> p m h w", m=2, h=2)
                v.tensor_copy(key_t[:, :, c * P:c * P + n], both[:, 0, :, 0:n])
                v.tensor_copy(low_t[:, :, c * P:c * P + n], both[:, 1, :, 0:n]).then_inc(key_kept, 1)
            v.wait_ge(key_kept, CHUNKS)

            def build_hots(b):
                with v.Fori(0, QT) as q:
                    for r in range(QW):
                        w = b * BW + q * QW + r
                        v.wait_ge(window_built, w + 1)
                        for h in range(2):
                            v.tensor_scalar(low_hot[:, r % 2, h, :], iota16[:, 0:P], low_t[:, h, bass.ds(w, 1)],
                                            None, ALU.is_equal)
                        for h in range(2):
                            hot = v.tensor_scalar(key_hot[:, r % 2, h, :], iota16[:, :], key_t[:, h, bass.ds(w, 1)],
                                                  None, ALU.is_equal)
                        hot.then_inc(hots_ready, 1)

            def scale_block(b, s, layer):
                nodes = bass.ds(b * GB, GB)
                v.wait_ge(block_summed, b + (BLOCKS * layer + 3))
                v.scalar_tensor_tensor(hT[:, nodes], pa[:, s, 0:GB], unscale, dis[:, nodes],
                                       op0=ALU.mult, op1=ALU.mult).then_inc(block_scaled, 1)

            slow = flag(v, 1)
            base = steps[0]
            with v.If(slow == 0):
                for layer in range(GCN_LAYERS):
                    for c in range(CHUNKS):
                        v.wait_ge(g_full, 2 * CHUNKS * layer + c + 1)
                        v.tensor_reduce(gmax[:, c:c + 1], pw_t if c % 2 else pb_t, AX.XY, ALU.max,
                                        apply_absolute_value=True).then_inc(g_seen, 1)
                    v.wait_ge(g_seen, CHUNKS * (layer + 1))
                    then(v.tensor_reduce(gtop, gmax, AX.X, ALU.max))
                    v.tensor_scalar(gtop, gtop, 1e-30, None, ALU.max).then_inc(top_ready, 1)
                    v.wait_ge(top_reduced, layer + 1)
                    then(v.tensor_scalar(power.bitcast(I32), gtop_all.bitcast(I32), 0x7F800000, None, ALU.bitwise_and))
                    then(v.tensor_scalar(unscale, power, 2.0 ** -13, None, ALU.mult))
                    v.reciprocal(scale, unscale).then_inc(scale_ready, 1)
                    v.wait_ge(scale_ready, layer + 1)
                    for c in range(CHUNKS):
                        v.wait_ge(high_ready, CHUNKS * layer + c + 1)
                        tiles = slice(c * CT, (c + 1) * CT)
                        v.scalar_tensor_tensor(g16[:, 1, tiles, :], pw_t if c % 2 else pb_t, scale, g16[:, 0, tiles, :],
                                               op0=ALU.mult, op1=ALU.subtract).then_inc(low_ready, 1)
                    if layer == 0:
                        build_hots(0)
                        with v.Fori(0, BLOCKS // 2 - 1) as c:
                            for s in range(2):
                                build_hots(c * 2 + (s + 1))
                                scale_block(c * 2 + s, s, 0)
                        build_hots(BLOCKS - 1)
                        scale_block(BLOCKS - 2, 0, 0)
                        scale_block(BLOCKS - 1, 1, 0)
                    else:
                        with v.Fori(0, BLOCKS // 2) as c:
                            for s in range(2):
                                scale_block(c * 2 + s, s, layer)
                v.wait_ge(block_scaled, BLOCKS * GCN_LAYERS + 2)
                then(v.memset(acc[:, NODES:ACC], 0.0))
            with v.Else():
                for d in range(GCN_LAYERS):
                    if d == 0:
                        v.memset(acc[:, NODES:ACC], 0.0)
                    else:
                        with v.Fori(0, CHUNKS) as c:
                            v.wait_ge(relued, c + (CHUNKS * (d - 1) + 1))
                            v.tensor_tensor(hT[:, bass.ds(c * CN, CN)], hT[:, bass.ds(c * CN, CN)],
                                            dis[:, bass.ds(c * CN, CN)], ALU.mult).then_inc(h_ready, 1)
                    v.wait_ge(gcn.term_ready, CHUNKS * (d + 1))
                    aggregate_wide(gcn, d, False)
                    with v.Fori(0, CHUNKS) as c:
                        v.tensor_tensor(hT[:, bass.ds(c * CN, CN)], acc[:, bass.ds(c * CN, CN)],
                                        dis[:, bass.ds(c * CN, CN)], ALU.mult).then_inc(scaled, 1)
                v.wait_ge(scaled, CHUNKS * GCN_LAYERS)
                v.sem_inc(dve_step, steps[0] - base)

            with v.Fori(0, CHUNKS) as c:
                then_ = loop_chain(c, 7)
                v.wait_ge(a_full, c * 2 + (CHUNKS + 1))
                then_(v.tensor_reduce(mx, pa_t, AX.X, ALU.max))
                v.tensor_tensor(z, pa_t, over_features(mx), ALU.subtract).then_inc(z_ready, 1)
                v.wait_ge(z_ready, c + 1)
                v.sem_inc(a_free, 1)
                v.wait_ge(exp_done, c + 1)
                v.tensor_reduce(ssum, e, AX.X, ALU.add).then_inc(s_ready, 1)
                v.wait_ge(x_back, 16)
                then_(v.tensor_tensor(z, z, xres[:, bass.ds(c * CT, CT), :], ALU.add))
                v.wait_ge(ln_done, c + 1)
                then_(v.tensor_tensor(z, z, over_features(lnsum), ALU.subtract))
                normalise(c, c, then_).then_inc(x1_ready, 1)
                v.wait_ge(x1_ready, c + 1)
            for d in range(REL_LAYERS):
                v.wait_ge(rel.term_ready, CHUNKS * (d + 1))
                with v.If(sparse_slow == 0):
                    aggregate_windows(rel, d, True)
                with v.Else():
                    aggregate_wide(rel, d, True)
                v.sem_inc(summed_all, 1)

            with v.Fori(0, CHUNKS) as c:
                then_ = loop_chain(c, 4)
                v.wait_ge(a_full, c + (CHUNKS * 3 + 1))
                v.tensor_tensor(z, pa_t, xres[:, bass.ds(c * CT, CT), :], ALU.add).then_inc(z_ready, 1)
                v.wait_ge(z_ready, c + (CHUNKS + 1))
                v.sem_inc(a_free, 1)
                normalise(c, c + CHUNKS, then_).then_inc(out_ready, 1)
                v.wait_ge(out_ready, c + 1)

        @block.tensor
        def _(pe):
            for ring in (deg, gcn, rel):
                pe.sem_inc(ring.group_summed, U)
            pe.sem_inc(window_built, 2)
            pe.sem_inc(block_summed, 2)
            pe.sem_inc(piece_used, 2 * PIECES)
            pe.wait_ge(ones_ready, 3)
            pe.matmul(pc[:, 0, 0:GROUPS], ones[0:1, :], e_all[0:1, 0:GROUPS], start=True, stop=True)\
              .then_inc(first_spread, 1)
            pe.wait_ge(inwin_ready, 1)
            pe.matmul(pc[0:1, 1, 0:1], inwin[:, 0:1], ones[:, 0:1], start=True, stop=True)\
              .then_inc(inwin_summed, 1)
            sparse_slow = flag(pe, 0)

            def summed_windows(ring, n):
                with pe.Fori(0, TURNS) as i:
                    for u in range(U):
                        pe.wait_ge(ring.window_added, i * U + (GROUPS * n + u + 1))
                        pe.wait_ge(ring.onehot_ready, i * U + (GROUPS * n + u + 1))
                        for q in range(G):
                            k = u * G + q
                            if ring is deg:
                                mm = pe.matmul(window(u), ones_b[:, :], onehot_b[:, u, q, :],
                                               start=(q == 0), stop=(q == G - 1))
                            else:
                                pe.wait_ge(ring.row_landed[k], i * 16 + 16 * (TURNS * n + 1))
                                mm = pe.matmul(window(u), rows[:, k, :], onehot[:, u, q, :],
                                               start=(q == 0), stop=(q == G - 1))
                        mm.then_inc(ring.group_summed, 1)

            def summed_wide(ring, n):
                with pe.Fori(0, TURNS) as i:
                    for u in range(U):
                        if ring is not deg:
                            for q in range(G):
                                pe.wait_ge(ring.row_landed[u * G + q], i * 16 + 16 * (TURNS * n + 1))
                        pe.nop(nofuse=True)
                        with pe.Fori(0, WIDES) as b:
                            step = (i * U + (u + GROUPS * n)) * WIDES + b
                            pe.wait_ge(ring.wide_added, step + 1)
                            pe.wait_ge(ring.wide_ready, step + 1)
                            for q in range(G):
                                mm = pe.matmul(pw[:, 0, :], ones[:, :] if ring is deg else rows[:, u * G + q, :],
                                               wide[:, q, :], start=(q == 0), stop=(q == G - 1))
                            mm.then_inc(ring.wide_summed, 1)
                        pe.wait_ge(ring.wide_summed, (i * U + (u + GROUPS * n + 1)) * WIDES)
                        pe.sem_inc(ring.group_summed, 1)

            def transpose_chunk(n, tile_of, c):
                pe.wait_ge(a_free, n + 1)
                for j in range(CT):
                    t = pe.transpose(pa_t[:, j, :], tile_of(c, j), ident[:, :])
                t.then_inc(a_full, 1)

            def node_tile(c, j):
                return hT[:, c * CN + j * P:c * CN + (j + 1) * P]

            def row_tile(c, j):
                return xres[:, c * CT + j, :]

            def own_term(c, n, w, full, free):
                pe.wait_ge(free, n + 1)
                for a in range(2):
                    mm = pe.matmul(pc[:, a, 0:HALF], w, hT[:, c * CN + a * HALF:c * CN + (a + 1) * HALF],
                                   start=True, stop=True)
                mm.then_inc(full, 1)

            def rel_rows_of(c, d):
                for j in range(CT):
                    pe.wait_ge(bt_free, c * CT + (NODE_TILES * d + j + (2 if j == 0 else 1)))
                    pe.matmul(pb[:, j % 2, :], node_tile(c, j), wr[:, d, :, :].rearrange("p r f -> p (r f)"),
                              start=True, stop=True).then_inc(bt_full, 1)

            with pe.If(sparse_slow == 0):
                summed_windows(deg, 0)
            with pe.Else():
                summed_wide(deg, 0)
            pe.wait_ge(cnt_ready, 1)
            for c in range(CHUNKS):
                mm = pe.matmul(pc[:, 0, c:c + 1], cnt_row[:, c * P:(c + 1) * P], ones[0:1, 0:1], start=True, stop=True)
            mm.then_inc(cnt_spread, 1)
            pe.wait_ge(pre_ready, 1)
            pe.wait_ge(consts_made, 6)
            pe.matmul(pc[:, 1, 0:CHUNKS], before[:, :], cnt, start=True, stop=False)
            pe.matmul(pc[:, 1, 0:CHUNKS], ones[:, :], pre, start=False, stop=True).then_inc(start_ready, 1)
            pe.wait_ge(loaded_x, 16)
            pe.wait_ge(loaded_w, 16 * 6)
            for c in range(CHUNKS):
                transpose_chunk(c, row_tile, c)
            pe.wait_ge(keys_ready, 1)
            pe.wait_ge(a_free, CHUNKS + 1)
            pe.wait_ge(inwin_ready, 2)
            pe.matmul(pc[0:1, 1, 0:1], inwin[:, 1:2], ones[:, 0:1], start=True, stop=True)\
              .then_inc(inwin_summed, 1)
            key = dstw.bitcast(F32)
            for c in range(CHUNKS):
                if c >= 2:
                    pe.wait_ge(key_kept, c - 1)
                for m, arr in enumerate((key, low)):
                    for h in range(2):
                        at = c * DE + h * P
                        t = pe.transpose(pa[:, c % 2, (m * 2 + h) * P:(m * 2 + h + 1) * P], arr[:, at:at + P], ident[:, :])
                t.then_inc(key_turned, 1)

            def table(layer, second):
                for c in range(CHUNKS):
                    if not second:
                        if layer == 0:
                            pe.wait_ge(x_scaled, c + 1)
                        else:
                            pe.wait_ge(block_next, BLOCKS * (layer - 1) + 2 * c + 2)
                        if c >= 2:
                            pe.wait_ge(g_seen, CHUNKS * layer + c - 1)
                    elif c < 2:
                        pe.wait_ge(g_seen, CHUNKS * (layer + 1))
                    else:
                        pe.wait_ge(high_ready, CHUNKS * layer + c - 1)
                        pe.wait_ge(low_ready, CHUNKS * layer + c - 1)
                    for j in range(CT):
                        mm = pe.matmul((pw_t if c % 2 else pb_t)[:, j, :], node_tile(c, j), wg[:, layer, :],
                                       start=True, stop=True)
                    mm.then_inc(g_full, 1)

            def begin_block(c, s, layer):
                b = c * 2 + s
                pe.wait_ge(block_scaled, b + (BLOCKS * layer + 1))
                pe.matmul(pa[:, s, 0:GB], ident16[:, :], zeros16, start=True, stop=False, skip_group_check=True)

            def end_block(c, s):
                for part in range(2):
                    at = 0
                    while at < GB:
                        j, off = divmod(s * GB + at, P)
                        n = min(P - off, GB - at)
                        mm = pe.matmul(pa[:, s, at:at + n],
                                       g16[:, part, bass.ds(c * CT + j, 1), :].rearrange("p a f -> p (a f)"),
                                       ident16[:, off:off + n], start=False, stop=(part == 1), skip_group_check=True)
                        at += n
                mm.then_inc(block_summed, 1)

            def build_block(b, beside=None):
                for part in range(2):
                    with pe.Fori(0, QT // 2) as q7:
                        for r in range(QW):
                            w = b * BW + q7 * QW + (part * (BW // 2) + r)
                            if r % 2 == 0:
                                pe.wait_ge(pair_kept, b * (BW // 2) + q7 * (QW // 2) + (part * (BW // 4) + r // 2 + 1))
                            pe.wait_ge(hots_ready, w + 1)
                            bank = pw if r < 2 else pb
                            for h in range(2):
                                mm = pe.matmul(bank[:, r % 2, 0:DKEYS], low_hot[:, r % 2, h, :], key_hot[:, r % 2, h, :],
                                               start=(h == 0), stop=(h == 1))
                            mm.then_inc(window_built, 1)
                        if beside is not None:
                            c, s = beside
                            for t in range(PIECE):
                                hi = bass.ds(q7 * PIECE + t, 1)
                                pe.matmul(pa[:, s, 0:GB], g16[:, part, hi, :].rearrange("p a f -> p (a f)"),
                                          a_blocks[:, s, hi, :].rearrange("p a n -> p (a n)"),
                                          start=False, stop=False, skip_group_check=True)

            def first_layer_begin(c, s):
                pe.wait_ge(pair_kept, (c * 2 + (s + 1)) * (BW // 2) + 2)
                begin_block(c, s, 0)

            slow = flag(pe, 1)
            with pe.If(slow == 0):
                pe.wait_ge(key_kept, CHUNKS)
                for layer in range(GCN_LAYERS):
                    table(layer, False)
                    table(layer, True)
                    pe.wait_ge(high_ready, CHUNKS * (layer + 1))
                    pe.wait_ge(low_ready, CHUNKS * (layer + 1))
                    if layer == 0:
                        build_block(0)
                        with pe.Fori(0, BLOCKS // 2 - 1) as c:
                            for s in range(2):
                                first_layer_begin(c, s)
                                build_block(c * 2 + (s + 1), (c, s))
                                end_block(c, s)
                        c = BLOCKS // 2 - 1
                        first_layer_begin(c, 0)
                        build_block(BLOCKS - 1, (c, 0))
                        end_block(c, 0)
                        first_layer_begin(c, 1)
                        for part in range(2):
                            for h in range(NODE_TILES):
                                pe.matmul(pa[:, 1, 0:GB], g16[:, part, h, :], a_blocks[:, 1, h, :],
                                          start=False, stop=False, skip_group_check=True)
                        end_block(c, 1)
                    else:
                        with pe.Fori(0, BLOCKS // 2) as c:
                            for s in range(2):
                                begin_block(c, s, layer)
                                for k in range(PIECES):
                                    pe.wait_ge(piece_landed[s * PIECES + k], c * 16 + 16 * ((layer - 1) * (BLOCKS // 2) + 1))
                                    for h in range(k * PIECE, (k + 1) * PIECE):
                                        for part in range(2):
                                            mm = pe.matmul(pa[:, s, 0:GB], g16[:, part, h, :], a_blocks[:, s, h, :],
                                                           start=False, stop=False, skip_group_check=True)
                                    mm.then_inc(piece_used, 1)
                                end_block(c, s)
            with pe.Else():
                for d in range(GCN_LAYERS):
                    for c in range(CHUNKS):
                        if d == 0:
                            pe.wait_ge(x_scaled, c + 1)
                        else:
                            pe.wait_ge(h_ready, CHUNKS * (d - 1) + c + 1)
                        pe.wait_ge(b_free, CHUNKS * d + c + 1)
                        for j in range(CT):
                            mm = pe.matmul(pb_t[:, j, :], node_tile(c, j), wg[:, d, :], start=True, stop=True)
                        mm.then_inc(b_full, 1)
                        own_term(c, c + CHUNKS * d, wg[:, d, :], c_full, c_free)
                    summed_wide(gcn, d)

            pe.wait_ge(h3_ready, 1)
            for c in range(CHUNKS):
                transpose_chunk(c * 2 + CHUNKS, node_tile, c)
                pe.wait_ge(x1_ready, c + 1)
                transpose_chunk(c * 2 + (CHUNKS + 1), row_tile, c)
                pe.wait_ge(in_ready, c + 1)
                rel_rows_of(c, 0)
                own_term(c, c, rr[:, 0, :], cr_full, cr_free)
            for d in range(REL_LAYERS):
                with pe.If(sparse_slow == 0):
                    summed_windows(rel, d)
                with pe.Else():
                    summed_wide(rel, d)
                if d == 0:
                    for c in range(CHUNKS):
                        pe.wait_ge(in_ready, c + CHUNKS + 1)
                        rel_rows_of(c, 1)
                        own_term(c, c + CHUNKS, rr[:, 1, :], cr_full, cr_free)
            pe.wait_ge(summed_all, REL_LAYERS)
            for c in range(CHUNKS):
                transpose_chunk(c + CHUNKS * 3, lambda c, j: acc[:, c * CN + j * P:c * CN + (j + 1) * P], c)


def kernel(x, src, dst, edge_type_4, edge_weight, L0_gnn_W0, L0_gnn_W1, L0_gnn_W2, L0_gnn_b0, L0_gnn_b1, L0_gnn_b2,
           L1_gnn_W1, L1_gnn_root1, L1_gnn_b1, L1_gnn_W2, L1_gnn_root2, L1_gnn_b2):
    import numpy as np
    import concourse.bacc as bacc
    from concourse.bass_utils import run_bass_kernel_spmd

    def by_tile(a, pad):
        a = np.asarray(a)
        a = np.concatenate([a, np.full(TILES * P - N_EDGES, pad, a.dtype)])
        return np.ascontiguousarray(a.reshape(TILES, P).T)

    def by_skip(a, pad):
        a = np.concatenate([np.asarray(a), np.full(SKIP_ROWS * SKIP + DE - N_EDGES, pad, a.dtype)])
        return np.ascontiguousarray(np.lib.stride_tricks.sliding_window_view(a, DE)[:SKIP_ROWS * SKIP:SKIP])

    src, dst = np.asarray(src), np.asarray(dst)
    weight = np.asarray(edge_weight)
    firsts = np.concatenate([dst[::G * P], np.zeros(GROUPS, dst.dtype)])[:GROUPS]
    xp = np.concatenate([np.asarray(x), np.zeros((NODES - N_NODES, F), np.float32)])
    arrays = {
        "x": xp,
        "src": by_tile(src, 0),
        "dst": by_tile(dst, -1),
        "src_slots": by_skip(src, 0),
        "dst_slots": by_skip(dst, -1),
        "first_dst": np.ascontiguousarray(firsts[None, :]),
        "edge_type": by_tile(edge_type_4, 0),
        "weight": by_tile(weight, weight[-1]),
        "gcn_w": np.stack([np.asarray(w) for w in (L0_gnn_W0, L0_gnn_W1, L0_gnn_W2)]),
        "gcn_b": np.stack([np.asarray(b) for b in (L0_gnn_b0, L0_gnn_b1, L0_gnn_b2)], axis=1),
        "rel_w1": np.asarray(L1_gnn_W1),
        "rel_w2": np.asarray(L1_gnn_W2),
        "rel_root": np.stack([np.asarray(L1_gnn_root1), np.asarray(L1_gnn_root2)]),
        "rel_b": np.stack([np.asarray(L1_gnn_b1), np.asarray(L1_gnn_b2)], axis=1),
    }
    nc = bacc.Bacc("TRN2", target_bir_lowering=False, num_devices=1)
    args = {n: nc.dram_tensor(f"in_{n}", a.shape, mybir.dt.from_np(a.dtype), kind="ExternalInput").ap()
            for n, a in arrays.items()}
    out = nc.dram_tensor("out_0", (N_NODES, F), F32, kind="ExternalOutput").ap()
    build(nc, out=out, **args)
    r = run_bass_kernel_spmd(nc, [{f"in_{n}": a for n, a in arrays.items()}], core_ids=[0])
    return r.results[0]["out_0"]
```

```python
from contextlib import ExitStack

import concourse.bass as bass
from concourse import mybir

P = 128
N_NODES = 6250
N_EDGES = 106250
F = 128
R = 4
GCN_LAYERS = 3
REL_LAYERS = 2

NODE_TILES = -(-N_NODES // P)
NODES = NODE_TILES * P
CT = 7
CHUNKS = NODE_TILES // CT
CN = CT * P
BESIDE = CT - 2
HALF = CN // 2
LAST_ROWS = N_NODES - (NODE_TILES - 1) * P

G = 4
U = 4
SLOTS = G * U
TURNS = -(-N_EDGES // (P * SLOTS))
GROUPS = TURNS * U
TILES = TURNS * SLOTS
WIN = 64
WIDE = 512
WIDES = -(-NODES // WIDE)
ACC = WIDES * WIDE

EARLY = CHUNKS - 1
EARLY_TURN = TURNS - EARLY

DW = 4
DWINS = NODES // DW
WCOLS = -(-DWINS // P)
DKEYS = DW * NODE_TILES
DE = 128
SKIP = 16
SKIP_ROWS = N_EDGES // SKIP + 1
GB = HALF
BLOCKS = NODES // GB
PAIR = 2 * DW
BW = GB // PAIR
QW = 4
QT = BW // QW
PIECE = 7
PIECES = NODE_TILES // PIECE

LO = 64
HI = NODES // LO
HI_CHUNK = CN // LO
LO_WINS = LO // DW
COLUMN_HIS = P // LO_WINS

EPS = 1e-5

F32 = mybir.dt.float32
F16 = mybir.dt.float16
I32 = mybir.dt.int32
ALU = mybir.AluOpType
ACT = mybir.ActivationFunctionType
AX = mybir.AxisListType


class Ring:

    def __init__(self, sem, name, windows):
        self.group_summed = sem(name + "_group_summed")
        self.wide_ready = sem(name + "_wide_ready")
        self.wide_summed = sem(name + "_wide_summed")
        self.wide_added = sem(name + "_wide_added")
        if windows:
            self.onehot_ready = sem(name + "_onehot_ready")
            self.window_added = sem(name + "_window_added")
            self.hot_built = sem(name + "_hot_built")
            self.wide_built = sem(name + "_wide_built")
        self.idx_ready = sem(name + "_idx_ready")
        self.row_landed = [sem(f"{name}_row_landed{k}") for k in range(SLOTS)]
        self.term_ready = sem(name + "_term_ready")


def build(nc, x, src, dst, slots, first_dst, edge_type, weight, gcn_w, gcn_b, rel_w1, rel_w2,
          rel_root, rel_b, out):
    gcn_table = nc.dram_tensor("gcn_table", [NODES, F], F32, kind="Internal").ap()
    rel_tables = [nc.dram_tensor(f"rel_table{d}", [NODES * R, F], F32, kind="Internal").ap()
                  for d in range(REL_LAYERS)]
    a_dram = nc.dram_tensor("a_dram", [BLOCKS, P, NODE_TILES * GB], F16, kind="Internal").ap()

    ctx = ExitStack()
    with ctx:
        def sb(name, shape, dt=F32):
            return ctx.enter_context(nc.sbuf_tensor(name, shape, dt))

        def sem(name):
            return ctx.enter_context(nc.semaphore(name))

        src_i = sb("src_i", [P, TILES], I32)
        rel_i = sb("rel_i", [P, TILES], I32)
        dst_f = sb("dst_f", [P, TILES])
        off_f = sb("off_f", [P, TILES])
        w_f = sb("w_f", [P, TILES])
        first_i = sb("first_i", [1, GROUPS], I32)
        big = sb("big", [P, NODE_TILES * GB])
        a_blocks = big[:, :].bitcast(F16).rearrange("p (s h n) -> p s h n", s=2, h=NODE_TILES)
        acc = big[:, 0:ACC]
        xres = big[:, ACC:ACC + NODES].rearrange("p (t f) -> p t f", f=F)
        tab = big[:, ACC + NODES:ACC + 2 * NODES]
        gcn_rows = tab.rearrange("p (t f) -> p t f", f=F)
        rel_rows = tab[:, 0:CT * R * F].rearrange("p (t f) -> p t f", f=R * F)
        slots_i = tab[:, 0:WCOLS * 2 * DE].bitcast(I32)
        srcw = slots_i.rearrange("p (c e) -> p c e", e=2 * DE)[:, :, 0:DE]
        dstw = slots_i.rearrange("p (c e) -> p c e", e=2 * DE)[:, :, DE:2 * DE]
        key = tab[:, 0:WCOLS * 2 * DE].rearrange("p (c e) -> p c e", e=2 * DE)[:, :, DE:2 * DE]
        low = tab[:, WCOLS * 2 * DE:WCOLS * 3 * DE].rearrange("p (c e) -> p c e", e=DE)
        turn_words = (HI + LO) * SLOTS // 2
        hist = big[:, 0:2 * turn_words].bitcast(F16).rearrange("p (s n k) -> p s n k", s=2, k=SLOTS)
        hi_hot, lo_hot = hist[:, :, 0:HI, :], hist[:, :, HI:HI + LO, :]
        hist_iota = big[:, 2 * turn_words:2 * turn_words + HI * SLOTS // 2].bitcast(F16)\
            .rearrange("p (n k) -> p n k", k=SLOTS)
        hi_lo = big[:, 2 * turn_words + HI * SLOTS // 2:2 * turn_words + HI * SLOTS // 2 + TILES].bitcast(F16)
        hi_t, lo_t = hi_lo[:, 0:TILES], hi_lo[:, TILES:2 * TILES]
        hT = sb("hT", [P, NODES])
        type_i = rel_i[:, :]
        wide = hT[:, 0:G * WIDE].rearrange("p (q n) -> p q n", q=G)
        dis = sb("dis", [P, NODES])
        g16 = sb("g16", [P, 2, NODE_TILES, F], F16)
        idx = sb("idx", [P, SLOTS], I32)
        rows_all = sb("rows", [P, SLOTS * F])
        rows = rows_all[:, :].rearrange("p (k f) -> p k f", f=F)
        low_t = rows_all[:, 0:DWINS // 2].bitcast(F16)
        low_hot = rows_all[:, DWINS // 2:DWINS // 2 + P * 2 * QW].bitcast(F16).rearrange("p (t n k) -> p t n k", t=2, k=2 * QW)
        zeros16 = rows_all[:, SLOTS * F - GB // 2:SLOTS * F].bitcast(F16)
        hot_all = sb("onehot", [P, U * G * WIN])
        onehot = hot_all[:, :].rearrange("p (u q n) -> p u q n", u=U, q=G)
        key_hot = [at[:, 0:QW * DKEYS].bitcast(F16).rearrange("p (w n) -> p w n", w=2 * QW)
                   for at in (hot_all, src_i)]
        work = sb("work", [P, 2 * CN])
        z_all, e_all = work[:, 0:CN], work[:, CN:2 * CN]
        iota_i = work[:, 0:WIDE].bitcast(I32)
        hist_sum = work[:, 0:LO]
        hist_dis = work[:, LO + P:2 * LO + P]
        cnt_hot = work[:, LO:LO + P]
        key_t = work[:, 0:DWINS]
        iota = sb("iota", [P, WIDE])
        iota16 = sb("iota16", [P, DKEYS], F16)
        wstart = sb("wstart", [P, WIDES])
        w4_i = sb("w4_i", [P, WCOLS], I32)
        ident = sb("ident", [P, P])
        ident16 = sb("ident16", [P, P], F16)
        before = sb("before", [P, P])
        ones = sb("ones", [P, P])
        mask_i = sb("mask_i", [P, COLUMN_HIS + WCOLS], I32)
        masks = sb("masks", [P, COLUMN_HIS + WCOLS])
        wg = sb("wg", [P, GCN_LAYERS, F])
        bg = sb("bg", [P, GCN_LAYERS])
        wr = sb("wr", [P, REL_LAYERS, R, F])
        low_iota = wr[:, 1, :, :].rearrange("p r f -> p (r f)").bitcast(F16)\
            .rearrange("p (n k) -> p n k", k=2 * QW)
        rr = sb("rr", [P, REL_LAYERS, F])
        br = sb("br", [P, REL_LAYERS])
        mx, ssum, lnsum, mean, var, rstd = (tab[:, CT * R * F + k * NODE_TILES:CT * R * F + (k + 1) * NODE_TILES]
                                            for k in range(6))
        tiny = sb("tiny", [P, 64])
        ext, ext_all = tiny[:, 0:2], tiny[:, 2:4]
        span = tiny[:, 4:8]
        inwin = tiny[:, 8:10]
        cnt, pre = tiny[:, 10:23], tiny[:, 23:36]
        hmax, wmax = tiny[:, 10:17], tiny[:, 17:17 + GCN_LAYERS]
        hi_cnt = tiny[:, 48:48 + LO_WINS]
        gtop, gtop_all = tiny[:, 43:44], tiny[:, 44:45]
        power, scale, unscale = tiny[:, 45:46], tiny[:, 46:47], tiny[:, 47:48]
        block_i = sb("block_i", [P, 16], I32)
        slow_i = sb("slow_i", [1, 2], I32)

        pa = ctx.enter_context(nc.psum_tensor("pa", [P, 2, 512], F32))
        pb = ctx.enter_context(nc.psum_tensor("pb", [P, 2, 512], F32))
        pc = ctx.enter_context(nc.psum_tensor("pc", [P, 2, 512], F32))
        pw = ctx.enter_context(nc.psum_tensor("pw", [P, 2, 512], F32))

        def tiles_of(bank):
            return bank[:, :, :].rearrange("p a n -> p (a n)")[:, 0:CN].rearrange("p (t f) -> p t f", f=F)
        pa_t, pb_t, pc_t, pw_t = tiles_of(pa), tiles_of(pb), tiles_of(pc), tiles_of(pw)

        def turned(c):
            return pw_t if c % 2 else pa_t

        def own_sums(c):
            return pa if c % 2 else pc

        def turned_sums(c):
            return pa_t if c % 2 else pc_t

        def z_of(c):
            return acc[:, c * CN:(c + 1) * CN].rearrange("p (t f) -> p t f", f=F)

        def e_of(c):
            return (e_all if c % 2 else z_all).rearrange("p (t f) -> p t f", f=F)

        def xres_of(c):
            return xres[:, c * CT:(c + 1) * CT, :]

        def of_chunk(stat, c):
            return stat[:, c * CT:(c + 1) * CT]

        rows_bank = (pb, pa)

        def table_bank(c):
            return (pb_t, pw_t, pc_t)[c % 3]

        def window(u):
            return (pw if u < 2 else pb)[:, u % 2, 0:WIN]

        gcn = Ring(sem, "gcn", windows=False)
        rel = Ring(sem, "rel", windows=True)
        loaded_dst = sem("loaded_dst")
        hist_hot = sem("hist_hot")
        hist_used = sem("hist_used")
        hist_ready = sem("hist_ready")
        hist_kept = sem("hist_kept")
        dis_masked = sem("dis_masked")
        dis_spread = sem("dis_spread")
        x_turned = sem("x_turned")
        x_kept = sem("x_kept")
        summed_all = sem("summed_all")
        loaded_edges = sem("loaded_edges")
        loaded_x = sem("loaded_x")
        loaded_w = sem("loaded_w")
        consts_made = sem("consts_made")
        dve_step = sem("dve_step")
        ones_ready = sem("ones_ready")
        ext_ready = sem("ext_ready")
        ext_reduced = sem("ext_reduced")
        first_spread = sem("first_spread")
        inwin_ready = sem("inwin_ready")
        inwin_summed = sem("inwin_summed")
        flag_ready = sem("flag_ready")
        root_ready = sem("root_ready")
        dis_ready = sem("dis_ready")
        cnt_ready = sem("cnt_ready")
        cnt_spread = sem("cnt_spread")
        pre_ready = sem("pre_ready")
        start_ready = sem("start_ready")
        block_ready = sem("block_ready")
        slots_landed = sem("slots_landed")
        keys_ready = sem("keys_ready")
        key_turned = sem("key_turned")
        key_kept = sem("key_kept")
        rows_turned = sem("rows_turned")
        x_scaled = sem("x_scaled")
        hots_ready = sem("hots_ready")
        window_built = sem("window_built")
        pair_kept = sem("pair_kept")
        loops_added = sem("loops_added")
        block_stored = sem("block_stored")
        block_safe = sem("block_safe")
        piece_landed = gcn.row_landed[0:2 * PIECES]
        piece_used = sem("piece_used")
        g_full = sem("g_full")
        top_ready = sem("top_ready")
        top_summed = sem("top_summed")
        scale_ready = sem("scale_ready")
        high_ready = sem("high_ready")
        low_ready = sem("low_ready")
        block_summed = sem("block_summed")
        block_scaled = sem("block_scaled")
        block_relued = sem("block_relued")
        block_next = sem("block_next")
        scaled = sem("scaled")
        relued = sem("relued")
        h_ready = sem("h_ready")
        b_full = sem("b_full")
        b_free = sem("b_free")
        c_full = sem("c_full")
        c_free = sem("c_free")
        rows_filled = sem("rows_filled")
        rows_stored = sem("rows_stored")
        h3_ready = sem("h3_ready")
        loaded_w2 = sem("loaded_w2")
        x_back = sem("x_back")
        in_ready = sem("in_ready")
        bt_full = sem("bt_full")
        bt_free = sem("bt_free")
        own_summed = sem("own_summed")
        rel_filled = sem("rel_filled")
        rel_stored = [sem(f"rel_stored{j}") for j in range(CT)]
        rel_free = sem("rel_free")
        z_ready = sem("z_ready")
        exp_done = sem("exp_done")
        s_ready = sem("s_ready")
        x_added = sem("x_added")
        ln_done = sem("ln_done")
        y_ready = sem("y_ready")
        sq_done = sem("sq_done")
        v_ready = sem("v_ready")
        sd_done = sem("sd_done")
        rstd_ready = sem("rstd_ready")
        x1_ready = sem("x1_ready")
        out_ready = sem("out_ready")
        out_stored = sem("out_stored")

        def flag(eng, which):
            eng.wait_ge(flag_ready, 1)
            return eng.value_load(slow_i[0:1, which:which + 1], min_val=0, max_val=N_EDGES)

        block = ctx.enter_context(nc.Block())

        @block.sync
        def _(sp):
            sp.sem_inc(rel_free, CT)
            sp.sem_inc(block_safe, 2)
            sp.dma_start(dst_f[:, :].bitcast(I32), dst).then_inc(loaded_dst, 16)
            sp.dma_start(first_i[:, :], first_dst).then_inc(loaded_dst, 16)
            sp.dma_start(w_f[:, :], weight).then_inc(loaded_edges, 16)
            sp.dma_start(src_i[:, :], src).then_inc(loaded_edges, 16)
            sp.dma_start(type_i, edge_type).then_inc(loaded_edges, 16)
            sp.dma_start(xres, x.rearrange("(t p) f -> p t f", p=P)).then_inc(loaded_x, 16)
            sp.dma_start(wg[:, :, :], gcn_w.rearrange("l i o -> i l o")).then_inc(loaded_w, 16)
            sp.dma_start(bg[:, :], gcn_b).then_inc(loaded_w, 16)
            sp.dma_start(wr[:, 0, :, :], rel_w1.rearrange("r i o -> i r o")).then_inc(loaded_w, 16)
            sp.dma_start(rr[:, :, :], rel_root.rearrange("l i o -> i l o")).then_inc(loaded_w, 16)
            sp.dma_start(br[:, :], rel_b).then_inc(loaded_w, 16)

            slow = flag(sp, 1)
            with sp.If(slow == 0):
                with sp.Fori(0, BLOCKS // 2) as c:
                    for s in range(2):
                        b = c * 2 + s
                        sp.wait_ge(loops_added, b + 1)
                        sp.dma_start(a_dram[bass.ds(b, 1)].rearrange("a p n -> (a p) n"),
                                     a_blocks[:, s].rearrange("p h n -> p (h n)")).then_inc(block_stored, 16)
                        sp.wait_ge(block_stored, b * 16 + 16)
                        sp.sem_inc(block_safe, 1)
                for layer in range(1, GCN_LAYERS):
                    with sp.Fori(0, BLOCKS // 2) as c:
                        for s in range(2):
                            if layer == 1:
                                sp.wait_ge(block_summed, 2 + BLOCKS - 1 + s)
                            for k in range(PIECES):
                                if k < PIECES - 1:
                                    n = ((layer - 1) * BLOCKS + s) * (PIECES - 1) + k
                                    sp.wait_ge(piece_used, c * (2 * (PIECES - 1)) + (n + 1))
                                else:
                                    sp.wait_ge(block_summed, c * 2 + (BLOCKS * layer + s + 1))
                                sp.dma_start(
                                    a_blocks[:, s, k * PIECE:(k + 1) * PIECE, :].rearrange("p h n -> p (h n)"),
                                    a_dram[bass.ds(c * 2 + s, 1), :, k * PIECE * GB:(k + 1) * PIECE * GB]
                                    .rearrange("a p n -> (a p) n"),
                                ).then_inc(piece_landed[s * PIECES + k], 16)
            with sp.Else():
                gcn_out = gcn_table.rearrange("(c t p) f -> c p t f", p=P, t=CT)
                for d in range(GCN_LAYERS):
                    with sp.Fori(0, CHUNKS) as c:
                        sp.wait_ge(rows_filled, c + (CHUNKS * d + 1))
                        sp.dma_start(gcn_out[bass.ds(c, 1)].rearrange("a p t f -> p (a t) f"),
                                     gcn_rows[:, bass.ds(c * CT, CT), :]).then_inc(rows_stored, 16)
                sp.wait_ge(rows_stored, 16 * CHUNKS * GCN_LAYERS)

            sp.wait_ge(h3_ready, 1)
            sp.dma_start(xres, x.rearrange("(t p) f -> p t f", p=P)).then_inc(x_back, 16)
            sp.dma_start(wr[:, 1, :, :], rel_w2.rearrange("r i o -> i r o")).then_inc(loaded_w2, 16)
            for d in range(REL_LAYERS):
                rel_out = rel_tables[d].rearrange("(c t p r) f -> (c t) p (r f)", p=P, t=CT, r=R)
                with sp.Fori(0, CHUNKS) as c:
                    for j in range(CT):
                        sp.wait_ge(rel_filled, c * CT + (NODE_TILES * d + j + 1))
                        sp.dma_start(rel_out[bass.ds(c * CT + j, 1)].rearrange("a p f -> (a p) f"),
                                     rel_rows[:, j, :]).then_inc(rel_stored[j], 16)
                    for j in range(CT):
                        sp.wait_ge(rel_stored[j], c * 16 + 16 * (CHUNKS * d + 1))
                        sp.sem_inc(rel_free, 1)
            out_v = out[0:(NODE_TILES - 1) * P, :].rearrange("(t p) f -> p t f", p=P)
            with sp.Fori(0, CHUNKS - 1) as c:
                sp.wait_ge(out_ready, c + 1)
                sp.dma_start(out_v[:, bass.ds(c * CT, CT), :], xres[:, bass.ds(c * CT, CT), :])\
                  .then_inc(out_stored, 16)
            sp.wait_ge(out_ready, CHUNKS)
            t0 = (CHUNKS - 1) * CT
            sp.dma_start(out_v[:, t0:NODE_TILES - 1, :], xres[:, t0:NODE_TILES - 1, :]).then_inc(out_stored, 16)
            sp.dma_start(out[(NODE_TILES - 1) * P:N_NODES, :], xres[0:LAST_ROWS, NODE_TILES - 1, :])\
              .then_inc(out_stored, 16)
            sp.wait_ge(out_stored, 16 * (CHUNKS + 1))

        @block.gpsimd
        def _(pool):
            pool.iota(iota_i, pattern=[[1, WIDE]], base=0, channel_multiplier=0).then_inc(consts_made, 1)
            pool.iota(w4_i[:, :], pattern=[[P * DW, WCOLS]], base=0, channel_multiplier=DW).then_inc(consts_made, 1)
            pool.memset(ident[:, :], 0.0).then_inc(consts_made, 1)
            pool.memset(before[:, :], 1.0).then_inc(consts_made, 1)
            pool.iota(mask_i[:, 0:COLUMN_HIS], pattern=[[-1, COLUMN_HIS]], base=0, channel_multiplier=1)\
                .then_inc(consts_made, 1)
            pool.iota(mask_i[:, COLUMN_HIS:], pattern=[[-COLUMN_HIS, WCOLS]], base=0, channel_multiplier=1)\
                .then_inc(consts_made, 1)
            pool.wait_ge(consts_made, 6)
            pool.affine_select(out=ident[:, :], in_=ident[:, :], compare_op=ALU.not_equal, fill=1.0,
                               base=0, pattern=[[-1, P]], channel_multiplier=1).then_inc(consts_made, 1)
            pool.affine_select(out=before[:, :], in_=before[:, :], compare_op=ALU.is_gt, fill=0.0,
                               base=0, pattern=[[1, P]], channel_multiplier=-1).then_inc(consts_made, 1)

            pool.wait_ge(block_ready, 1)
            for c in range(WCOLS):
                pool.indirect_dma_start(
                    out=slots_i[:, c * 2 * DE:(c + 1) * 2 * DE], out_offset=None, in_=slots,
                    in_offset=bass.IndirectOffsetOnAxis(ap=block_i[:, c:c + 1], axis=0),
                ).then_inc(slots_landed, 16)

            pool.wait_ge(x_kept, CHUNKS)
            for c in range(CHUNKS):
                nodes = slice(c * CN, (c + 1) * CN)
                pool.wait_ge(dis_ready, c + 1)
                pool.tensor_tensor(hT[:, nodes], hT[:, nodes], dis[:, nodes], ALU.mult).then_inc(x_scaled, 1)
            pool.wait_ge(ext_ready, 1)
            pool.partition_all_reduce(ext_all, ext, P, bass.bass_isa.ReduceOp.max).then_inc(ext_reduced, 1)

            def gather(table, ring, n):
                with pool.Fori(0, TURNS) as i:
                    for k in range(SLOTS):
                        if k % (SLOTS // 2) == 0:
                            pool.wait_ge(ring.idx_ready, i * 2 + (2 * TURNS * n + k // (SLOTS // 2) + 1))
                        if k % G == 0:
                            pool.wait_ge(ring.group_summed, i * U + (GROUPS * n + k // G + 1))
                            pool.nop(nofuse=True)
                        pool.indirect_dma_start(
                            out=rows[:, k, :], out_offset=None, in_=table,
                            in_offset=bass.IndirectOffsetOnAxis(ap=idx[:, k:k + 1], axis=0),
                        ).then_inc(ring.row_landed[k], 16)

            slow = flag(pool, 1)
            with pool.If(slow == 0):
                def next_input(b, layer):
                    nodes = bass.ds(b * GB, GB)
                    pool.wait_ge(block_relued, b + (BLOCKS * layer + 1))
                    pool.tensor_tensor(hT[:, nodes], hT[:, nodes], dis[:, nodes], ALU.mult)\
                        .then_inc(block_next, 1)

                def add_loops(c, s):
                    b = c * 2 + s
                    pool.wait_ge(pair_kept, b * (BW // 2) + (2 + BW // 2))
                    at = 0
                    while at < GB:
                        j, off = divmod(s * GB + at, P)
                        n = min(P - off, GB - at)
                        tile = a_blocks[:, s, bass.ds(c * CT + j, 1), at:at + n].rearrange("p a n -> p (a n)")
                        add = pool.tensor_tensor(tile, tile, ident16[:, off:off + n], ALU.add)
                        at += n
                    add.then_inc(loops_added, 1)

                for s in range(2):
                    add_loops(0, s)
                with pool.Fori(1, BLOCKS // 2) as c:
                    for s in range(2):
                        next_input(c * 2 - 2 + s, 0)
                        add_loops(c, s)
                for b in range(BLOCKS - 2, BLOCKS):
                    next_input(b, 0)
                for layer in range(1, GCN_LAYERS - 1):
                    with pool.Fori(0, BLOCKS) as b:
                        next_input(b, layer)
            with pool.Else():
                pool.wait_ge(key_kept, CHUNKS)
                for layer in range(GCN_LAYERS):
                    pool.wait_ge(rows_stored, 16 * CHUNKS * (layer + 1))
                    gather(gcn_table, gcn, layer)
            pool.wait_ge(x_back, 16)
            for c in range(CHUNKS):
                pool.wait_ge(exp_done, c + 1)
                pool.tensor_tensor(z_of(c), z_of(c), xres_of(c), ALU.add).then_inc(x_added, 1)
            for d in range(REL_LAYERS):
                pool.wait_ge(rel_free, CT + NODE_TILES * (d + 1))
                gather(rel_tables[d], rel, d)

        @block.scalar
        def _(act):
            act.sem_inc(pair_kept, 2)
            act.sem_inc(b_free, 1)
            act.sem_inc(bt_free, 2)
            act.sem_inc(c_free, 1)
            act.wait_ge(loaded_edges, 16 * 3)
            act.wait_ge(loaded_w, 16 * 5)

            def activation(out_, in_, func, **kw):
                act.nop(nofuse=True)
                return act.activation(out_, in_, func, **kw)

            act.wait_ge(hist_kept, 1)
            act.activation(hist_dis[0:HI, :], hist_sum[0:HI, :], ACT.Sqrt, bias=ones[0:HI, 0:1])\
               .then_inc(root_ready, 1)
            for c in range(CHUNKS):
                act.wait_ge(x_turned, c + 1)
                act.activation(hT[:, c * CN:(c + 1) * CN].rearrange("p (t n) -> p t n", n=P), pw_t if c % 2 else pa_t,
                               ACT.Copy).then_inc(x_kept, 1)
            for c in range(CHUNKS):
                act.wait_ge(dis_spread, c + 1)
                act.activation(dis[:, c * CN:(c + 1) * CN].rearrange("p (a n) -> p a n", a=2),
                               (pw if c % 2 else pb)[:, :, 0:HALF], ACT.Copy).then_inc(dis_ready, 1)

            def copy_indices(table_rows, ring, n, first=0, last=TURNS):
                half = SLOTS // 2
                with act.Fori(first, last) as i:
                    for h in range(2):
                        act.wait_ge(ring.group_summed, i * U + (GROUPS * n + (h + 1) * U // 2))
                        activation(idx[:, h * half:(h + 1) * half],
                                   table_rows[:, bass.ds(i * SLOTS + h * half, half)], ACT.Copy)\
                            .then_inc(ring.idx_ready, 1)

            def own_term(c, n):
                act.wait_ge(c_full, n + 1)
                nodes = acc[:, bass.ds(c * CN, CN)].rearrange("p (a n) -> p a n", a=2)
                activation(nodes, pc[:, :, 0:HALF], ACT.Copy).then_inc(gcn.term_ready, 1)
                act.wait_ge(gcn.term_ready, n + 1)
                act.sem_inc(c_free, 1)

            def relu_block(b, layer):
                nodes = bass.ds(b * GB, GB)
                act.wait_ge(block_scaled, b + (BLOCKS * layer + 3))
                activation(hT[:, nodes], hT[:, nodes], ACT.Relu, bias=bg[:, layer:layer + 1])\
                    .then_inc(block_relued, 1)

            def keep_turn(b, s, q):
                for k, bank in enumerate((pw, pb)):
                    act.wait_ge(window_built, (b * BW + q * QW) + (2 * QW + 2 * k + 2))
                    at = a_blocks[:, s, :, bass.ds(q * (QW * PAIR) + k * 2 * PAIR, 2 * PAIR)]
                    activation(at.rearrange("p h (w d) -> p w h d", w=2),
                               bank[:, :, 0:2 * DKEYS].rearrange("p w (d h) -> p w h d", d=PAIR), ACT.Copy)\
                        .then_inc(pair_kept, 1)

            def keep_block(b, s, relu_before=False):
                act.wait_ge(block_summed, b + 1)
                act.wait_ge(block_safe, b + 1)
                for q in range(2):
                    keep_turn(b, s, q)
                if relu_before:
                    relu_block(b - 2, 0)
                with act.Fori(2, QT) as q:
                    keep_turn(b, s, q)

            slow = flag(act, 1)
            with act.If(slow == 0):
                for layer in range(GCN_LAYERS):
                    act.wait_ge(scale_ready, layer + 1)
                    for c in range(CHUNKS):
                        act.wait_ge(g_full, CHUNKS * layer + c + 1)
                        activation(g16[:, 0, c * CT:(c + 1) * CT, :], table_bank(c), ACT.Identity,
                                   scale=scale).then_inc(high_ready, 1)
                    if layer == 0:
                        keep_block(0, 0)
                        keep_block(1, 1)
                        with act.Fori(1, BLOCKS // 2) as c:
                            for s in range(2):
                                keep_block(c * 2 + s, s, True)
                        relu_block(BLOCKS - 2, 0)
                        relu_block(BLOCKS - 1, 0)
                    else:
                        with act.Fori(0, BLOCKS) as b:
                            relu_block(b, layer)
                act.wait_ge(block_relued, BLOCKS * GCN_LAYERS)
            with act.Else():
                for d in range(GCN_LAYERS):
                    with act.Fori(0, CHUNKS) as c:
                        chunk = hT[:, bass.ds(c * CN, CN)]
                        if d > 0:
                            act.wait_ge(scaled, c + (CHUNKS * (d - 1) + 1))
                            activation(chunk, chunk, ACT.Relu, bias=bg[:, d - 1:d]).then_inc(relued, 1)
                        act.wait_ge(b_full, c + (CHUNKS * d + 1))
                        activation(gcn_rows[:, bass.ds(c * CT, CT), :], pb_t, ACT.Copy).then_inc(rows_filled, 1)
                        act.wait_ge(rows_filled, c + (CHUNKS * d + 1))
                        act.sem_inc(b_free, 1)
                        own_term(c, c + CHUNKS * d)
                    copy_indices(src_i, gcn, d)
                with act.Fori(0, CHUNKS) as c:
                    chunk = hT[:, bass.ds(c * CN, CN)]
                    act.wait_ge(scaled, c + (CHUNKS * (GCN_LAYERS - 1) + 1))
                    activation(chunk, chunk, ACT.Relu, bias=bg[:, GCN_LAYERS - 1:GCN_LAYERS]).then_inc(relued, 1)
                act.wait_ge(relued, CHUNKS * GCN_LAYERS)
            act.sem_inc(h3_ready, 1)

            def rel_rows_out(c, d, beside=None):
                for j in range(CT):
                    if j == BESIDE and beside is not None:
                        beside()
                    act.wait_ge(bt_full, c * CT + (NODE_TILES * d + j + 1))
                    act.wait_ge(rel_free, c * CT + (NODE_TILES * d + j + 1))
                    activation(rel_rows[:, j, :], rows_bank[d][:, j % 2, :], ACT.Copy).then_inc(rel_filled, 1)
                    act.wait_ge(rel_filled, c * CT + (NODE_TILES * d + j + 1))
                    act.sem_inc(bt_free, 1)

            def squares(c, n):
                act.wait_ge(y_ready, n + 1)
                act.activation(e_of(c), z_of(c), ACT.Square).then_inc(sq_done, 1)

            def root(c, n):
                act.wait_ge(v_ready, n + 1)
                act.activation(of_chunk(rstd, c), of_chunk(var, c), ACT.Sqrt).then_inc(sd_done, 1)

            def turn_back(c):
                act.wait_ge(rows_turned, CHUNKS + c + 1)
                act.activation(hT[:, c * CN:(c + 1) * CN].rearrange("p (t n) -> p t n", n=P), turned(c), ACT.Copy)\
                   .then_inc(in_ready, 1)

            for c in range(CHUNKS):
                act.wait_ge(z_ready, c + 1)
                if c >= 2:
                    act.wait_ge(s_ready, c - 1)
                act.activation(e_of(c), z_of(c), ACT.Exp).then_inc(exp_done, 1)
            act.wait_ge(s_ready, CHUNKS)
            act.activation(lnsum, ssum, ACT.Ln).then_inc(ln_done, 1)
            squares(0, 0)
            root(0, 0)
            squares(1, 1)
            turn_back(0)
            for c in range(CHUNKS):
                if c + 1 < CHUNKS:
                    root(c + 1, c + 1)
                if c + 2 < CHUNKS:
                    squares(c + 2, c + 2)
                rel_rows_out(c, 0, None if c + 1 == CHUNKS else lambda: turn_back(c + 1))
            sparse_slow = flag(act, 0)
            with act.If(sparse_slow == 0):
                copy_indices(rel_i, rel, 0, 0, EARLY_TURN + 1)
                for c in range(EARLY):
                    if c + 1 < EARLY:
                        copy_indices(rel_i, rel, 0, EARLY_TURN + c + 1, EARLY_TURN + c + 2)
                    rel_rows_out(c, 1)
            with act.Else():
                copy_indices(rel_i, rel, 0)
                for c in range(EARLY):
                    rel_rows_out(c, 1)
            rel_rows_out(EARLY, 1)

            def scale_rows(c):
                act.wait_ge(rstd_ready, c + 1)
                for j in range(CT):
                    t = c * CT + j
                    a = act.activation(xres[:, t, :], z_of(c)[:, j, :], ACT.Copy, scale=rstd[:, t:t + 1])
                a.then_inc(out_ready, 1)

            def last_norm(c):
                squares(c, CHUNKS + c)
                root(c, CHUNKS + c)
                scale_rows(c)

            with act.If(sparse_slow == 0):
                copy_indices(rel_i, rel, 1, 0, EARLY_TURN + 1)
                for c in range(EARLY):
                    last_norm(c)
                    if c + 1 < EARLY:
                        copy_indices(rel_i, rel, 1, EARLY_TURN + c + 1, EARLY_TURN + c + 2)
            with act.Else():
                copy_indices(rel_i, rel, 1)
                for c in range(EARLY):
                    last_norm(c)
            last_norm(EARLY)

        @block.vector
        def _(v):
            steps = [0]

            def then(ins):
                steps[0] += 1
                ins.then_inc(dve_step, 1)
                v.wait_ge(dve_step, steps[0])

            v.sem_inc(block_scaled, 2)
            v.sem_inc(rel.window_added, U)
            for ring in (gcn, rel):
                v.sem_inc(ring.wide_added, 1)
            v.memset(ones[:, :], 1.0).then_inc(ones_ready, 1)
            then(v.memset(zeros16, 0.0))
            v.wait_ge(consts_made, 8)
            then(v.tensor_copy(iota[:, :], iota_i))
            then(v.tensor_scalar(wstart[:, :], iota_i[:, 0:WIDES], float(WIDE), None, ALU.mult))
            then(v.tensor_copy(iota16[:, :], iota[:, 0:DKEYS]))
            then(v.tensor_copy(hist_iota, iota[:, 0:HI].unsqueeze(2).to_broadcast([P, HI, SLOTS])))

            v.wait_ge(loaded_dst, 16 * 2)
            then(v.tensor_copy(e_all[0:1, 0:GROUPS], first_i[:, :]))
            v.sem_inc(ones_ready, 1)
            dst_i, part_i = dst_f[:, :].bitcast(I32), off_f[:, :].bitcast(I32)
            then(v.tensor_scalar(part_i, dst_i, LO.bit_length() - 1, None, ALU.arith_shift_right))
            then(v.tensor_copy(hi_t, part_i))
            then(v.tensor_scalar(part_i, dst_i, LO - 1, None, ALU.bitwise_and))
            then(v.tensor_copy(lo_t, part_i))
            with v.Fori(0, TURNS // 2) as i:
                for s in range(2):
                    tiles = bass.ds((i * 2 + s) * SLOTS, SLOTS)
                    v.wait_ge(hist_used, i * 2 + (s + 1))
                    v.tensor_tensor(hi_hot[:, s], hist_iota, hi_t[:, tiles].unsqueeze(1).to_broadcast([P, HI, SLOTS]),
                                    ALU.is_equal)
                    v.tensor_tensor(lo_hot[:, s], hist_iota[:, 0:LO],
                                    lo_t[:, tiles].unsqueeze(1).to_broadcast([P, LO, SLOTS]), ALU.is_equal)\
                     .then_inc(hist_hot, 1)
            then(v.tensor_copy(ident16[:, :], ident[:, :]))
            then(v.tensor_copy(low_iota, iota[:, 0:P].unsqueeze(2).to_broadcast([P, P, 2 * QW])))
            then(v.tensor_scalar(mask_i[:, 0:COLUMN_HIS], mask_i[:, 0:COLUMN_HIS], COLUMN_HIS - 1, None,
                                 ALU.bitwise_and))
            then(v.tensor_scalar(mask_i[:, COLUMN_HIS:], mask_i[:, COLUMN_HIS:], COLUMN_HIS.bit_length() - 1, None,
                                 ALU.logical_shift_right))
            then(v.tensor_scalar(masks[:, :], mask_i[:, :], 0.0, None, ALU.is_equal))
            v.wait_ge(first_spread, 1)
            then(v.tensor_copy(e_all[:, 0:GROUPS], pc[:, 1, 0:GROUPS]))

            v.wait_ge(hist_ready, 1)
            v.tensor_copy(hist_sum[0:HI, :], pb[0:HI, 0, 0:LO]).then_inc(hist_kept, 1)
            v.wait_ge(hist_kept, 1)
            then(v.tensor_reduce(hi_cnt[0:HI, :], hist_sum[0:HI, :].rearrange("p (w d) -> p w d", d=DW), AX.X, ALU.add))
            v.tensor_tensor(cnt_hot[0:HI, :].rearrange("p (a w) -> p a w", w=LO_WINS),
                            masks[0:HI, 0:COLUMN_HIS].unsqueeze(2).to_broadcast([HI, COLUMN_HIS, LO_WINS]),
                            hi_cnt[0:HI, :].unsqueeze(1).to_broadcast([HI, COLUMN_HIS, LO_WINS]), ALU.mult)\
             .then_inc(cnt_ready, 1)
            v.wait_ge(root_ready, 1)
            then(v.reciprocal(hist_dis[0:HI, :], hist_dis[0:HI, :]))
            v.wait_ge(cnt_spread, 1)
            then(v.tensor_copy(cnt, pc[:, 0, 0:WCOLS]))
            then(v.memset(pre[:, 0:1], 0.0))
            for k in range(1, WCOLS):
                then(v.tensor_tensor(pre[:, k:k + 1], pre[:, k - 1:k], cnt[:, k - 1:k], ALU.add))
            v.sem_inc(pre_ready, 1)
            v.wait_ge(start_ready, 1)
            then(v.tensor_copy(block_i[:, 0:WCOLS], pc[:, 1, 0:WCOLS]))
            v.tensor_scalar(block_i[:, 0:WCOLS], block_i[:, 0:WCOLS], SKIP.bit_length() - 1, None,
                            ALU.logical_shift_right).then_inc(block_ready, 1)

            for c in range(CHUNKS):
                v.tensor_tensor(dis[0:HI, c * CN:(c + 1) * CN].rearrange("p (h l) -> p h l", l=LO),
                                hist_dis[0:HI, :].unsqueeze(1).to_broadcast([HI, HI_CHUNK, LO]),
                                ident[0:HI, c * HI_CHUNK:(c + 1) * HI_CHUNK].unsqueeze(2).to_broadcast([HI, HI_CHUNK, LO]),
                                ALU.mult).then_inc(dis_masked, 1)
            then(v.tensor_copy(off_f[:, :], dst_i))
            then(v.tensor_copy(dst_f[:, :], off_f[:, :]))
            then(v.tensor_tensor(off_f[:, :].rearrange("p (g k) -> p g k", k=G),
                                 dst_f[:, :].rearrange("p (g k) -> p g k", k=G),
                                 e_all[:, 0:GROUPS].unsqueeze(2).to_broadcast([P, GROUPS, G]), ALU.subtract))
            then(v.tensor_scalar(z_all[:, 0:TILES], off_f[:, :], 0.0, None, ALU.is_ge))
            then(v.scalar_tensor_tensor(z_all[:, 0:TILES], off_f[:, :], float(WIN), z_all[:, 0:TILES],
                                        op0=ALU.is_lt, op1=ALU.mult))
            late = slice(EARLY_TURN * SLOTS, TILES)
            then(v.scalar_tensor_tensor(z_all[:, late], dst_f[:, late], float(EARLY * CN), z_all[:, late],
                                        op0=ALU.is_ge, op1=ALU.mult))
            then(v.tensor_reduce(inwin[:, 0:1], z_all[:, 0:TILES], AX.X, ALU.add))
            v.wait_ge(loaded_edges, 16 * 3)
            then(v.tensor_copy(z_all[:, 0:TILES], src_i[:, :]))
            then(v.tensor_copy(e_all[:, 0:TILES], type_i))
            then(v.scalar_tensor_tensor(rel_i[:, :], z_all[:, 0:TILES], float(R), e_all[:, 0:TILES],
                                        op0=ALU.mult, op1=ALU.add))
            then(v.tensor_reduce(ext[:, 0:1], w_f[:, :], AX.X, ALU.min))
            then(v.tensor_scalar(ext[:, 0:1], ext[:, 0:1], -1.0, None, ALU.mult))
            v.tensor_reduce(ext[:, 1:2], w_f[:, :], AX.X, ALU.max).then_inc(ext_ready, 1)

            def hots_of(ring, n, i, u):
                off = off_f[:, bass.ds(i * SLOTS + u * G, G)].unsqueeze(2).to_broadcast([P, G, WIN])
                nodes = iota[:, 0:WIN].unsqueeze(1).to_broadcast([P, G, WIN])
                v.wait_ge(ring.group_summed, i * U + (GROUPS * n + u + 1))
                v.tensor_tensor(onehot[:, u], off, nodes, ALU.is_equal).then_inc(ring.hot_built, 1)
                v.wait_ge(ring.hot_built, i * U + (GROUPS * n + u + 1))
                w = w_f[:, bass.ds(i * SLOTS + u * G, G)].unsqueeze(2).to_broadcast([P, G, WIN])
                v.tensor_tensor(onehot[:, u], onehot[:, u], w, ALU.mult).then_inc(ring.onehot_ready, 1)

            def load_firsts(i):
                return [v.value_load(first_i[0:1, bass.ds(i * U + u, 1)], min_val=0, max_val=N_NODES - 1)
                        for u in range(U)]

            def add_window(ring, n, first, i, u):
                nodes = acc[:, bass.ds(first, WIN)]
                v.wait_ge(ring.group_summed, i * U + (GROUPS * n + U + u + 1))
                v.wait_ge(ring.window_added, i * U + (GROUPS * n + U + u))
                v.tensor_tensor(nodes, nodes, window(u), ALU.add).then_inc(ring.window_added, 1)

            def aggregate_windows(ring, n, early):
                for u in range(U):
                    hots_of(ring, n, 0, u)

                def turn(i):
                    firsts = load_firsts(i - 1)
                    for u in range(U):
                        hots_of(ring, n, i, u)
                        add_window(ring, n, firsts[u], i - 1, u)

                with v.Fori(1, EARLY_TURN) as i:
                    turn(i)
                for c in range(EARLY):
                    turn(EARLY_TURN + c)
                    v.wait_ge(ring.window_added, (EARLY_TURN + c) * U + (GROUPS * n + U))
                    early(c)
                firsts = load_firsts(TURNS - 1)
                for u in range(U):
                    add_window(ring, n, firsts[u], TURNS - 1, u)
                v.wait_ge(ring.window_added, GROUPS * (n + 1) + U)

            def aggregate_wide(ring, n, weighted):
                done = GROUPS * n
                with v.Fori(0, GROUPS) as g:
                    with v.Fori(0, WIDES) as b:
                        dst_g = dst_f[:, bass.ds(g * G, G)].unsqueeze(2).to_broadcast([P, G, WIDE])
                        nodes = iota[:, :].unsqueeze(1).to_broadcast([P, G, WIDE])
                        step = g * WIDES + b + done * WIDES
                        hot = v.scalar_tensor_tensor(wide, nodes, wstart[:, bass.ds(b, 1)], dst_g,
                                                     op0=ALU.add, op1=ALU.is_equal)
                        if weighted:
                            w = w_f[:, bass.ds(g * G, G)].unsqueeze(2).to_broadcast([P, G, WIDE])
                            hot.then_inc(ring.wide_built, 1)
                            v.wait_ge(ring.wide_built, step + 1)
                            hot = v.tensor_tensor(wide, wide, w, ALU.mult)
                        hot.then_inc(ring.wide_ready, 1)
                        nodes = acc[:, bass.ds(b * WIDE, WIDE)]
                        v.wait_ge(ring.wide_summed, step + 1)
                        v.wait_ge(ring.wide_added, step + 1)
                        v.tensor_tensor(nodes, nodes, pw[:, 0, :], ALU.add).then_inc(ring.wide_added, 1)
                v.wait_ge(ring.wide_added, (done + GROUPS) * WIDES + 1)

            def over_features(stat, c):
                return of_chunk(stat, c).unsqueeze(2).to_broadcast([P, CT, F])

            def row_means(c):
                then(v.tensor_reduce(of_chunk(mean, c), z_of(c), AX.X, ALU.add))
                then(v.tensor_scalar(of_chunk(mean, c), of_chunk(mean, c), 1.0 / F, None, ALU.mult))

            def centre(c):
                v.tensor_tensor(z_of(c), z_of(c), over_features(mean, c), ALU.subtract).then_inc(y_ready, 1)

            def variances(c, n):
                v.wait_ge(sq_done, n + 1)
                then(v.tensor_reduce(of_chunk(var, c), e_of(c), AX.X, ALU.add))
                v.tensor_scalar(of_chunk(var, c), of_chunk(var, c), 1.0 / F, EPS, ALU.mult, ALU.add)\
                 .then_inc(v_ready, 1)

            def invert_roots(c, n):
                v.wait_ge(sd_done, n + 1)
                return v.reciprocal(of_chunk(rstd, c), of_chunk(rstd, c))

            def normalise(rows_in, n, scale_rows):
                for c in range(CHUNKS + 1):
                    if c < CHUNKS:
                        rows_in(c)
                        row_means(c)
                    if c > 0:
                        variances(c - 1, n + c - 1)
                    if c < CHUNKS:
                        centre(c)
                    if c > 0:
                        scale_rows(c - 1, invert_roots(c - 1, n + c - 1))

            def own_terms(d):
                for c in range(CHUNKS):
                    v.wait_ge(own_summed, CHUNKS * d + c + 1)
                    v.tensor_scalar(acc[:, c * CN:(c + 1) * CN].rearrange("p (a n) -> p a n", a=2),
                                    own_sums(c)[:, :, 0:HALF], br[:, d:d + 1], None, ALU.add)\
                     .then_inc(rel.term_ready, 1)
                v.wait_ge(rel.term_ready, CHUNKS * (d + 1))

            v.wait_ge(slots_landed, 16 * WCOLS)
            scratch = work[:, 0:WCOLS * DE].rearrange("p (c e) -> p c e", e=DE)
            scratch_i = work[:, 0:WCOLS * DE].bitcast(I32).rearrange("p (c e) -> p c e", e=DE)
            then(v.tensor_scalar(scratch_i, srcw, P - 1, None, ALU.bitwise_and))
            then(v.tensor_copy(low, scratch_i))
            then(v.tensor_scalar(srcw, srcw, P.bit_length() - 1, None, ALU.logical_shift_right))
            then(v.tensor_tensor(key, dstw, w4_i[:, :].unsqueeze(2).to_broadcast([P, WCOLS, DE]), ALU.subtract))
            then(v.scalar_tensor_tensor(key, key, float(NODE_TILES), srcw, op0=ALU.mult, op1=ALU.add))
            then(v.tensor_scalar(scratch, key, 0.0, None, ALU.is_ge))
            v.sem_inc(keys_ready, 1)
            then(v.scalar_tensor_tensor(scratch, key, float(DKEYS), scratch, op0=ALU.is_lt, op1=ALU.mult))
            v.tensor_reduce(inwin[:, 1:2], work[:, 0:WCOLS * DE], AX.X, ALU.add).then_inc(inwin_ready, 1)
            v.wait_ge(inwin_summed, 1)
            v.tensor_scalar(slow_i[0:1, :], pc[0:1, 1, 0:2], -1.0, float(N_EDGES), ALU.mult, ALU.add)\
             .then_inc(flag_ready, 1)
            def largest_of(chunks, layer):
                for c in chunks:
                    if layer == 0:
                        v.wait_ge(x_scaled, c + 1)
                    else:
                        v.wait_ge(block_next, BLOCKS * (layer - 1) + 2 * c + 2)
                    then(v.tensor_reduce(hmax[:, c:c + 1], hT[:, c * CN:(c + 1) * CN], AX.X, ALU.max,
                                         apply_absolute_value=True))

            for c in range(CHUNKS):
                at, n = c * 2 * P, min(2 * P, DWINS - c * 2 * P)
                v.wait_ge(key_turned, c + 1)
                v.tensor_copy(key_t[:, at:at + n], pa[:, c % 2, 0:n])
                v.tensor_copy(low_t[:, at:at + n], pa[:, c % 2, 2 * P:2 * P + n]).then_inc(key_kept, 1)
                largest_of([c], 0)
            v.wait_ge(key_kept, CHUNKS)

            v.wait_ge(ext_reduced, 1)
            then(v.tensor_tensor(span[:, 0:1], ext_all[:, 0:1], ext_all[:, 1:2], ALU.add))
            then(v.tensor_scalar(span[:, 1:2], span[:, 0:1], 1e-8, None, ALU.add))
            then(v.reciprocal(span[:, 2:3], span[:, 1:2]))
            then(v.tensor_scalar(w_f[:, :], w_f[:, :], ext_all[:, 0:1], span[:, 2:3], ALU.add, ALU.mult))

            def scale_block(b, s, layer):
                nodes = bass.ds(b * GB, GB)
                v.wait_ge(block_summed, b + (BLOCKS * layer + 3))
                v.scalar_tensor_tensor(hT[:, nodes], pa[:, s, 0:GB], unscale, dis[:, nodes],
                                       op0=ALU.mult, op1=ALU.mult).then_inc(block_scaled, 1)

            def turn_hots(w0, t):
                v.wait_ge(window_built, w0 + QW)
                v.tensor_tensor(low_hot[:, t], low_iota,
                                low_t[:, bass.ds(w0 * 2, 2 * QW)].unsqueeze(1).to_broadcast([P, P, 2 * QW]),
                                ALU.is_equal)
                for r in range(QW):
                    for h in range(2):
                        hot = v.tensor_scalar(key_hot[t][:, r * 2 + h, :], iota16[:, :],
                                              key_t[:, bass.ds(w0 * 2 + (r * 2 + h), 1)], None, ALU.is_equal)
                    hot.then_inc(hots_ready, 1)

            def build_hots(b, scale_before=None):
                for t in range(2):
                    turn_hots(b * BW + t * QW, t)
                if scale_before is not None:
                    scale_block(b - 2, scale_before, 0)
                with v.Fori(1, QT // 2) as q:
                    for t in range(2):
                        turn_hots(b * BW + q * (2 * QW) + t * QW, t)

            def last_blocks(layer):
                scale_block(BLOCKS - 2, 0, layer)
                if layer < GCN_LAYERS - 1:
                    largest_of(range(CHUNKS - 1), layer + 1)
                scale_block(BLOCKS - 1, 1, layer)
                if layer < GCN_LAYERS - 1:
                    largest_of([CHUNKS - 1], layer + 1)

            sparse_slow, slow = flag(v, 0), flag(v, 1)
            base = steps[0]
            with v.If(slow == 0):
                v.wait_ge(loaded_w, 16 * 5)
                then(v.tensor_reduce(wmax, wg[:, :, :], AX.X, ALU.max, apply_absolute_value=True))
                for layer in range(GCN_LAYERS):
                    then(v.tensor_reduce(gtop, hmax, AX.X, ALU.max))
                    v.tensor_tensor(gtop, gtop, wmax[:, layer:layer + 1], ALU.mult).then_inc(top_ready, 1)
                    v.wait_ge(top_summed, layer + 1)
                    then(v.tensor_scalar(gtop_all, pa[:, 0, 0:1], 1e-30, 1e36, ALU.max, ALU.min))
                    then(v.tensor_scalar(power.bitcast(I32), gtop_all.bitcast(I32), 0x7F800000, None, ALU.bitwise_and))
                    then(v.tensor_scalar(unscale, power, 2.0 ** -13, None, ALU.mult))
                    v.reciprocal(scale, unscale).then_inc(scale_ready, 1)
                    v.wait_ge(scale_ready, layer + 1)
                    for c in range(CHUNKS):
                        v.wait_ge(high_ready, CHUNKS * layer + c + 1)
                        tiles = slice(c * CT, (c + 1) * CT)
                        v.scalar_tensor_tensor(g16[:, 1, tiles, :], table_bank(c), scale, g16[:, 0, tiles, :],
                                               op0=ALU.mult, op1=ALU.subtract).then_inc(low_ready, 1)
                    if layer == 0:
                        build_hots(0)
                        build_hots(1)
                        with v.Fori(1, BLOCKS // 2) as c:
                            for s in range(2):
                                build_hots(c * 2 + s, s)
                    else:
                        with v.Fori(0, BLOCKS // 2 - 1) as c:
                            for s in range(2):
                                scale_block(c * 2 + s, s, layer)
                    last_blocks(layer)
                v.wait_ge(block_scaled, BLOCKS * GCN_LAYERS + 2)
                then(v.memset(acc[:, NODES:ACC], 0.0))
            with v.Else():
                for d in range(GCN_LAYERS):
                    if d == 0:
                        v.memset(acc[:, NODES:ACC], 0.0)
                    else:
                        with v.Fori(0, CHUNKS) as c:
                            v.wait_ge(relued, c + (CHUNKS * (d - 1) + 1))
                            v.tensor_tensor(hT[:, bass.ds(c * CN, CN)], hT[:, bass.ds(c * CN, CN)],
                                            dis[:, bass.ds(c * CN, CN)], ALU.mult).then_inc(h_ready, 1)
                    v.wait_ge(gcn.term_ready, CHUNKS * (d + 1))
                    aggregate_wide(gcn, d, False)
                    with v.Fori(0, CHUNKS) as c:
                        v.tensor_tensor(hT[:, bass.ds(c * CN, CN)], acc[:, bass.ds(c * CN, CN)],
                                        dis[:, bass.ds(c * CN, CN)], ALU.mult).then_inc(scaled, 1)
                v.wait_ge(scaled, CHUNKS * GCN_LAYERS)
                v.sem_inc(dve_step, steps[0] - base)

            for c in range(CHUNKS + 1):
                if c < CHUNKS:
                    v.wait_ge(rows_turned, c + 1)
                    then(v.tensor_reduce(of_chunk(mx, c), turned(c), AX.X, ALU.max))
                    v.tensor_tensor(z_of(c), turned(c), over_features(mx, c), ALU.subtract).then_inc(z_ready, 1)
                if c > 0:
                    v.wait_ge(exp_done, c)
                    v.tensor_reduce(of_chunk(ssum, c - 1), e_of(c - 1), AX.X, ALU.add).then_inc(s_ready, 1)

            def log_softmax_and_x(c):
                v.wait_ge(x_added, c + 1)
                v.wait_ge(ln_done, 1)
                then(v.tensor_tensor(z_of(c), z_of(c), over_features(lnsum, c), ALU.subtract))

            v.wait_ge(z_ready, CHUNKS)

            def scale_here(c, inverted):
                then(inverted)
                v.tensor_tensor(xres_of(c), z_of(c), over_features(rstd, c), ALU.mult).then_inc(x1_ready, 1)

            normalise(log_softmax_and_x, 0, scale_here)
            v.wait_ge(x1_ready, CHUNKS)
            v.wait_ge(loaded_w, 16 * 5)

            def relu_sums(c):
                nodes = slice(c * CN, (c + 1) * CN)
                v.tensor_scalar(hT[:, nodes], acc[:, nodes], 0.0, None, ALU.max).then_inc(in_ready, 1)

            def last_norm(c):
                v.wait_ge(rows_turned, CHUNKS * 2 + c + 1)
                then(v.tensor_tensor(z_of(c), turned_sums(c), xres_of(c), ALU.add))
                v.sem_inc(z_ready, 1)
                row_means(c)
                centre(c)
                variances(c, CHUNKS + c)
                invert_roots(c, CHUNKS + c).then_inc(rstd_ready, 1)

            for d, after in enumerate((relu_sums, last_norm)):
                own_terms(d)
                base = steps[0]
                with v.If(sparse_slow == 0):
                    aggregate_windows(rel, d, after)
                steps[0] = base
                with v.Else():
                    aggregate_wide(rel, d, True)
                    for c in range(EARLY):
                        after(c)
                v.sem_inc(summed_all, 1)
                after(EARLY)
                if d == 0:
                    v.wait_ge(in_ready, CHUNKS * 2)

        @block.tensor
        def _(pe):
            for ring in (gcn, rel):
                pe.sem_inc(ring.group_summed, U)
            pe.sem_inc(window_built, 2 * QW)
            pe.sem_inc(block_summed, 2)
            pe.sem_inc(piece_used, 2 * (PIECES - 1))
            pe.sem_inc(hist_used, 2)
            pe.wait_ge(ones_ready, 2)
            pe.matmul(pc[:, 1, 0:GROUPS], ones[0:1, :], e_all[0:1, 0:GROUPS], start=True, stop=True)\
              .then_inc(first_spread, 1)

            def zero_product(**kw):
                return pe.matmul(pb[0:HI, 0, 0:LO], zeros16[:, 0:HI], zeros16[:, 0:LO], skip_group_check=True, **kw)
            zero_product(start=True, stop=False)
            with pe.Fori(0, TURNS // 2) as i:
                for s in range(2):
                    pe.wait_ge(hist_hot, i * 2 + (s + 1))
                    for k in range(SLOTS):
                        mm = pe.matmul(pb[0:HI, 0, 0:LO], hi_hot[:, s, :, k], lo_hot[:, s, :, k],
                                       start=False, stop=False, skip_group_check=True)
                    mm.then_inc(hist_used, 1)
            zero_product(start=False, stop=True).then_inc(hist_ready, 1)

            def summed_windows(ring, n, before, after):
                def turn(i):
                    for u in range(U):
                        pe.wait_ge(ring.window_added, i * U + (GROUPS * n + u + 1))
                        pe.wait_ge(ring.onehot_ready, i * U + (GROUPS * n + u + 1))
                        for q in range(G):
                            k = u * G + q
                            pe.wait_ge(ring.row_landed[k], i * 16 + 16 * (TURNS * n + 1))
                            mm = pe.matmul(window(u), rows[:, k, :], onehot[:, u, q, :],
                                           start=(q == 0), stop=(q == G - 1))
                        mm.then_inc(ring.group_summed, 1)

                with pe.Fori(0, EARLY_TURN) as i:
                    turn(i)
                for c in range(EARLY):
                    before(c)
                    turn(EARLY_TURN + c)
                    after(c)

            def summed_wide(ring, n):
                with pe.Fori(0, TURNS) as i:
                    for u in range(U):
                        for q in range(G):
                            pe.wait_ge(ring.row_landed[u * G + q], i * 16 + 16 * (TURNS * n + 1))
                        pe.nop(nofuse=True)
                        with pe.Fori(0, WIDES) as b:
                            step = (i * U + (u + GROUPS * n)) * WIDES + b
                            pe.wait_ge(ring.wide_added, step + 1)
                            pe.wait_ge(ring.wide_ready, step + 1)
                            for q in range(G):
                                mm = pe.matmul(pw[:, 0, :], rows[:, u * G + q, :], wide[:, q, :],
                                               start=(q == 0), stop=(q == G - 1))
                            mm.then_inc(ring.wide_summed, 1)
                        pe.wait_ge(ring.wide_summed, (i * U + (u + GROUPS * n + 1)) * WIDES)
                        pe.sem_inc(ring.group_summed, 1)

            def transpose_chunk(tile_of, c):
                for j in range(CT):
                    t = pe.transpose(turned(c)[:, j, :], tile_of(c, j), ident[:, :])
                t.then_inc(rows_turned, 1)

            def node_tile(c, j):
                return hT[:, c * CN + j * P:c * CN + (j + 1) * P]

            def row_tile(c, j):
                return xres[:, c * CT + j, :]

            def own_term(c, bank, w):
                for a in range(2):
                    mm = pe.matmul(bank[:, a, 0:HALF], w, hT[:, c * CN + a * HALF:c * CN + (a + 1) * HALF],
                                   start=True, stop=True)
                return mm

            def rel_own_terms(d):
                for c in range(CHUNKS):
                    if c >= 2:
                        pe.wait_ge(rel.term_ready, CHUNKS * d + c - 1)
                    own_term(c, own_sums(c), rr[:, d, :]).then_inc(own_summed, 1)

            def rel_rows_of(c, d, beside=None):
                for j in range(CT):
                    if j == BESIDE and beside is not None:
                        beside()
                    pe.wait_ge(bt_free, c * CT + (NODE_TILES * d + j + (2 if j == 0 else 1)))
                    pe.matmul(rows_bank[d][:, j % 2, :], node_tile(c, j), wr[:, d, :, :].rearrange("p r f -> p (r f)"),
                              start=True, stop=True).then_inc(bt_full, 1)

            pe.wait_ge(cnt_ready, 1)
            pe.matmul(pc[:, 0, 0:WCOLS], cnt_hot[0:HI, :], masks[0:HI, COLUMN_HIS:], start=True, stop=True)\
              .then_inc(cnt_spread, 1)
            pe.wait_ge(pre_ready, 1)
            pe.matmul(pc[:, 1, 0:WCOLS], before[:, :], cnt, start=True, stop=False)
            pe.matmul(pc[:, 1, 0:WCOLS], ones[:, :], pre, start=False, stop=True).then_inc(start_ready, 1)
            pe.wait_ge(loaded_x, 16)
            pe.wait_ge(loaded_w, 16 * 5)
            for c in range(CHUNKS):
                if c >= 2:
                    pe.wait_ge(x_kept, c - 1)
                for j in range(CT):
                    t = pe.transpose((pw_t if c % 2 else pa_t)[:, j, :], row_tile(c, j), ident[:, :])
                t.then_inc(x_turned, 1)
            pe.wait_ge(x_kept, CHUNKS)
            for c in range(CHUNKS):
                if c >= 2:
                    pe.wait_ge(dis_ready, c - 1)
                pe.wait_ge(dis_masked, c + 1)
                for a in range(2):
                    at = c * CN + a * HALF
                    mm = pe.matmul((pw if c % 2 else pb)[:, a, 0:HALF], ones[0:HI, :], dis[0:HI, at:at + HALF],
                                   start=True, stop=True)
                mm.then_inc(dis_spread, 1)
            pe.wait_ge(keys_ready, 1)
            pe.wait_ge(inwin_ready, 1)
            for which in range(2):
                mm = pe.matmul(pc[0:1, 1, which:which + 1], inwin[:, which:which + 1], ones[:, 0:1],
                               start=True, stop=True)
            mm.then_inc(inwin_summed, 1)
            for c in range(CHUNKS):
                if c >= 2:
                    pe.wait_ge(key_kept, c - 1)
                for m, arr in enumerate((key, low)):
                    for h in range(min(2, WCOLS - 2 * c)):
                        t = pe.transpose(pa[:, c % 2, (m * 2 + h) * P:(m * 2 + h + 1) * P], arr[:, 2 * c + h, :],
                                         ident[:, :])
                t.then_inc(key_turned, 1)

            def table(layer):
                for c in range(CHUNKS):
                    if c == 3:
                        pe.wait_ge(top_ready, layer + 1)
                        pe.matmul(pa[:, 0, 0:1], ones[:, :], gtop, start=True, stop=True).then_inc(top_summed, 1)
                    if c >= 3:
                        pe.wait_ge(high_ready, CHUNKS * layer + c - 2)
                        pe.wait_ge(low_ready, CHUNKS * layer + c - 2)
                    if layer == 0:
                        pe.wait_ge(x_scaled, c + 1)
                    else:
                        pe.wait_ge(block_next, BLOCKS * (layer - 1) + 2 * c + 2)
                    for j in range(CT):
                        mm = pe.matmul(table_bank(c)[:, j, :], node_tile(c, j), wg[:, layer, :], start=True, stop=True)
                    mm.then_inc(g_full, 1)

            def first_layer_begin(b):
                pe.wait_ge(loops_added, b + 1)
                pe.wait_ge(block_scaled, b + 1)

            def products(part, his, s):
                for hi in his:
                    mm = pe.matmul(pa[:, s, 0:GB], g16[:, part, hi, :], a_blocks[:, s, hi, :],
                                   start=(part == 0 and hi == 0), stop=(part == 1 and hi == NODE_TILES - 1),
                                   skip_group_check=True)
                return mm

            def build_block(b, beside):
                for q in range(QT + 1):
                    part, of_part = divmod(q - 1, QT // 2)
                    for r in range(QW):
                        if q < QT:
                            if r % 2 == 0:
                                pe.wait_ge(pair_kept, b * (BW // 2) + (q * (QW // 2) + r // 2 + 1))
                            pe.wait_ge(hots_ready, b * BW + (q * QW + r + 1))
                            for h in range(2):
                                mm = pe.matmul((pw if r < 2 else pb)[:, r % 2, h * DKEYS:(h + 1) * DKEYS],
                                               low_hot[:, q % 2, :, r * 2 + h], key_hot[q % 2][:, r * 2 + h, :],
                                               start=True, stop=True)
                            mm.then_inc(window_built, 1)
                        if beside is not None and r % 2 == 1:
                            if q > 0:
                                first = of_part * PIECE
                                his = range(first, first + PIECE // 2 + 1) if r == 1 else \
                                    range(first + PIECE // 2 + 1, first + PIECE)
                                mm = products(part, his, beside)
                            elif r == QW - 1:
                                first_layer_begin(b - 1)
                if beside is not None:
                    mm.then_inc(block_summed, 1)

            pe.wait_ge(dis_ready, CHUNKS)
            sparse_slow, slow = flag(pe, 0), flag(pe, 1)
            with pe.If(slow == 0):
                pe.wait_ge(key_kept, CHUNKS)
                for layer in range(GCN_LAYERS):
                    table(layer)
                    pe.wait_ge(high_ready, CHUNKS * (layer + 1))
                    pe.wait_ge(low_ready, CHUNKS * (layer + 1))
                    if layer == 0:
                        build_block(0, None)
                        build_block(1, 0)
                        with pe.Fori(1, BLOCKS // 2) as c:
                            build_block(c * 2, 1)
                            build_block(c * 2 + 1, 0)
                        first_layer_begin(BLOCKS - 1)
                        for part in range(2):
                            mm = products(part, range(NODE_TILES), 1)
                        mm.then_inc(block_summed, 1)
                    else:
                        with pe.Fori(0, BLOCKS // 2) as c:
                            for s in range(2):
                                pe.wait_ge(block_scaled, c * 2 + (s + BLOCKS * layer + 1))
                                for k in range(PIECES):
                                    pe.wait_ge(piece_landed[s * PIECES + k], c * 16 + 16 * ((layer - 1) * (BLOCKS // 2) + 1))
                                    for h in range(k * PIECE, (k + 1) * PIECE):
                                        for part in range(2):
                                            mm = pe.matmul(pa[:, s, 0:GB], g16[:, part, h, :], a_blocks[:, s, h, :],
                                                           start=(h == 0 and part == 0),
                                                           stop=(h == NODE_TILES - 1 and part == 1),
                                                           skip_group_check=True)
                                    mm.then_inc(piece_used if k < PIECES - 1 else block_summed, 1)
            with pe.Else():
                for d in range(GCN_LAYERS):
                    for c in range(CHUNKS):
                        if d == 0:
                            pe.wait_ge(x_scaled, c + 1)
                        else:
                            pe.wait_ge(h_ready, CHUNKS * (d - 1) + c + 1)
                        pe.wait_ge(b_free, CHUNKS * d + c + 1)
                        for j in range(CT):
                            mm = pe.matmul(pb_t[:, j, :], node_tile(c, j), wg[:, d, :], start=True, stop=True)
                        mm.then_inc(b_full, 1)
                        pe.wait_ge(c_free, c + CHUNKS * d + 1)
                        own_term(c, pc, wg[:, d, :]).then_inc(c_full, 1)
                    summed_wide(gcn, d)

            pe.wait_ge(h3_ready, 1)
            for c in range(CHUNKS):
                if c >= 2:
                    pe.wait_ge(z_ready, c - 1)
                transpose_chunk(node_tile, c)

            def turn_norm(c):
                pe.wait_ge(x1_ready, c + 1)
                transpose_chunk(row_tile, c)

            turn_norm(0)
            for c in range(CHUNKS):
                pe.wait_ge(in_ready, c + 1)
                rel_rows_of(c, 0, None if c + 1 == CHUNKS else lambda: turn_norm(c + 1))
            rel_own_terms(0)

            def second_rows(c):
                pe.wait_ge(in_ready, c + CHUNKS + 1)
                rel_rows_of(c, 1)

            def turn_sums(c):
                if c >= 2:
                    pe.wait_ge(z_ready, CHUNKS + c - 1)
                for j in range(CT):
                    at = c * CN + j * P
                    t = pe.transpose(turned_sums(c)[:, j, :], acc[:, at:at + P], ident[:, :])
                t.then_inc(rows_turned, 1)

            def turn_sums_early(c):
                pe.wait_ge(rel.window_added, (EARLY_TURN + c) * U + (GROUPS + U))
                turn_sums(c)

            pe.wait_ge(loaded_w2, 16)
            with pe.If(sparse_slow == 0):
                summed_windows(rel, 0, lambda c: None, second_rows)
            with pe.Else():
                summed_wide(rel, 0)
                for c in range(EARLY):
                    second_rows(c)
            second_rows(EARLY)
            pe.wait_ge(bt_free, 2 + 2 * NODE_TILES)
            rel_own_terms(1)
            pe.wait_ge(rel.term_ready, 2 * CHUNKS)
            with pe.If(sparse_slow == 0):
                summed_windows(rel, 1, turn_sums_early, lambda c: None)
            with pe.Else():
                summed_wide(rel, 1)
                pe.wait_ge(rel.wide_added, 2 * GROUPS * WIDES + 1)
                for c in range(EARLY):
                    turn_sums(c)
            pe.wait_ge(summed_all, REL_LAYERS)
            turn_sums(EARLY)


def kernel(x, src, dst, edge_type_4, edge_weight, L0_gnn_W0, L0_gnn_W1, L0_gnn_W2, L0_gnn_b0, L0_gnn_b1, L0_gnn_b2,
           L1_gnn_W1, L1_gnn_root1, L1_gnn_b1, L1_gnn_W2, L1_gnn_root2, L1_gnn_b2):
    import numpy as np
    import concourse.bacc as bacc
    from concourse.bass_utils import run_bass_kernel_spmd

    def by_tile(a, pad):
        a = np.asarray(a)
        a = np.concatenate([a, np.full(TILES * P - N_EDGES, pad, a.dtype)])
        return np.ascontiguousarray(a.reshape(TILES, P).T)

    def by_skip(a, pad):
        a = np.concatenate([np.asarray(a), np.full(SKIP_ROWS * SKIP + DE - N_EDGES, pad, a.dtype)])
        return np.ascontiguousarray(np.lib.stride_tricks.sliding_window_view(a, DE)[:SKIP_ROWS * SKIP:SKIP])

    src, dst = np.asarray(src), np.asarray(dst)
    weight = np.asarray(edge_weight)
    firsts = np.concatenate([dst[::G * P], np.zeros(GROUPS, dst.dtype)])[:GROUPS]
    xp = np.concatenate([np.asarray(x), np.zeros((NODES - N_NODES, F), np.float32)])
    arrays = {
        "x": xp,
        "src": by_tile(src, 0),
        "dst": by_tile(dst, -1),
        "slots": np.concatenate([by_skip(src, 0), by_skip(dst, -1)], axis=1),
        "first_dst": np.ascontiguousarray(firsts[None, :]),
        "edge_type": by_tile(edge_type_4, 0),
        "weight": by_tile(weight, weight[-1]),
        "gcn_w": np.stack([np.asarray(w) for w in (L0_gnn_W0, L0_gnn_W1, L0_gnn_W2)]),
        "gcn_b": np.stack([np.asarray(b) for b in (L0_gnn_b0, L0_gnn_b1, L0_gnn_b2)], axis=1),
        "rel_w1": np.asarray(L1_gnn_W1),
        "rel_w2": np.asarray(L1_gnn_W2),
        "rel_root": np.stack([np.asarray(L1_gnn_root1), np.asarray(L1_gnn_root2)]),
        "rel_b": np.stack([np.asarray(L1_gnn_b1), np.asarray(L1_gnn_b2)], axis=1),
    }
    nc = bacc.Bacc("TRN2", target_bir_lowering=False, num_devices=1)
    args = {n: nc.dram_tensor(f"in_{n}", a.shape, mybir.dt.from_np(a.dtype), kind="ExternalInput").ap()
            for n, a in arrays.items()}
    out = nc.dram_tensor("out_0", (N_NODES, F), F32, kind="ExternalOutput").ap()
    build(nc, out=out, **args)
    r = run_bass_kernel_spmd(nc, [{f"in_{n}": a for n, a in arrays.items()}], core_ids=[0])
    return r.results[0]["out_0"]
```
